# Optimizing a Trainium2 kernel written in Bass

```python
import numpy as np
import jax
import jax.numpy as jnp

def _softmax(x, axis=-1):
    return jax.nn.softmax(x, axis=axis)

def _gelu(x):
    return jax.nn.gelu(x, approximate=True)

def _silu(x):
    return jax.nn.silu(x)

def _sigmoid(x):
    return jax.nn.sigmoid(x)

def _layernorm(x, axis=-1, eps=1e-05):
    m = jnp.mean(x, axis=axis, keepdims=True)
    v = jnp.var(x, axis=axis, keepdims=True)
    return (x - m) / jnp.sqrt(v + eps)

def _scatter_add(tgt, idx, src, axis=0):
    return tgt.at[idx].add(src)

def _segment_sum(src, seg, n):
    return jax.ops.segment_sum(src, seg, n)
kernel_name = 'mk_seq_postln_d2_jaxref_r8_73c77d'

def setup_inputs(seed: int=0):
    np.random.seed(seed)
    _w = jnp.asarray

    def _L0_attn_setup():
        import jax, jax.numpy as jnp
        import numpy as np
        N_HEADS = 16
        key = jax.random.key(seed)
        k1, k2, k3 = jax.random.split(key, 3)
        b, t, d = (2, 256, 128)
        x = jax.random.normal(k1, (b, t, d), dtype=jnp.float32)
        w_qkv = jax.random.normal(k2, (d, 3 * d), dtype=jnp.float32) * 0.02
        w_out = jax.random.normal(k3, (d, d), dtype=jnp.float32) * 0.02
        return {'x': x, 'w_qkv': w_qkv, 'w_out': w_out}
    _L0_attn_in = _L0_attn_setup()

    def _L0_ffn_setup():
        import jax, jax.numpy as jnp
        import numpy as np
        B, T, C = (4, 256, 128)
        E, H, K = (8, 256, 2)
        key = jax.random.key(seed)
        ks = jax.random.split(key, 7)
        s_in = 1.0 / np.sqrt(C)
        s_hid = 1.0 / np.sqrt(H)
        return {'x': jax.random.normal(ks[0], (B, T, C), dtype=jnp.float32), 'gate_w': jax.random.uniform(ks[1], (C, E), jnp.float32, -s_in, s_in), 'gate_b': jnp.zeros((E,), jnp.float32), 'w1': jax.random.uniform(ks[2], (E, C, H), jnp.float32, -s_in, s_in), 'b1': jax.random.uniform(ks[3], (E, H), jnp.float32, -s_in, s_in), 'w2': jax.random.uniform(ks[4], (E, H, C), jnp.float32, -s_hid, s_hid), 'b2': jax.random.uniform(ks[5], (E, C), jnp.float32, -s_hid, s_hid)}
    _L0_ffn_in = _L0_ffn_setup()

    def _L1_attn_setup():
        import jax, jax.numpy as jnp
        import numpy as np
        DIM = 128
        NUM_HEADS = 16
        HEAD_DIM = DIM // NUM_HEADS
        SCALE = HEAD_DIM ** (-0.5)
        key = jax.random.key(seed)
        ks = jax.random.split(key, 5)
        B, N, C = (2, 256, DIM)
        x = jax.random.normal(ks[0], (B, N, C), dtype=jnp.float32)
        w_in = jax.random.normal(ks[1], (3 * C, C), dtype=jnp.float32) * C ** (-0.5)
        b_in = jax.random.normal(ks[2], (3 * C,), dtype=jnp.float32) * 0.02
        w_out = jax.random.normal(ks[3], (C, C), dtype=jnp.float32) * C ** (-0.5)
        b_out = jax.random.normal(ks[4], (C,), dtype=jnp.float32) * 0.02
        return {'x': x, 'w_in': w_in, 'b_in': b_in, 'w_out': w_out, 'b_out': b_out}
    _L1_attn_in = _L1_attn_setup()

    def _L1_ffn_setup():
        import jax, jax.numpy as jnp
        import numpy as np
        S, B, D = (128, 2, 128)
        E, TOPK = (15, 3)
        F = 128
        FS = 256

        def _uinit(k, shape, out_dim):
            std = out_dim ** (-0.5)
            return jax.random.uniform(k, shape, jnp.float32, -std, std)
        key = jax.random.key(seed)
        ks = jax.random.split(key, 10)
        return {'x': jax.random.normal(ks[0], (S, B, D), jnp.float32), 'gate_w': jax.random.normal(ks[1], (E, D), jnp.float32) * D ** (-0.5), 'fc1_w': _uinit(ks[2], (E, 2 * F, D), 2 * F), 'fc1_b': _uinit(ks[3], (E, 2 * F), 2 * F), 'geglu_mult': jnp.ones((E, F), jnp.float32), 'fc2_w': _uinit(ks[4], (E, D, F), D), 'fc2_b': _uinit(ks[5], (E, D), D), 's_fc1_w': _uinit(ks[6], (2 * FS, D), 2 * FS), 's_fc1_b': _uinit(ks[7], (2 * FS,), 2 * FS), 's_geglu_mult': jnp.ones((FS,), jnp.float32), 's_fc2_w': _uinit(ks[8], (D, FS), D), 's_fc2_b': _uinit(ks[9], (D,), D)}
    _L1_ffn_in = _L1_ffn_setup()
    _d = {'L0_attn_x': _L0_attn_in['x'], 'L0_attn_w_qkv': _L0_attn_in['w_qkv'], 'L0_attn_w_out': _L0_attn_in['w_out'], 'L0_ffn_gate_w': _L0_ffn_in['gate_w'], 'L0_ffn_gate_b': _L0_ffn_in['gate_b'], 'L0_ffn_w1': _L0_ffn_in['w1'], 'L0_ffn_b1': _L0_ffn_in['b1'], 'L0_ffn_w2': _L0_ffn_in['w2'], 'L0_ffn_b2': _L0_ffn_in['b2'], 'L1_attn_w_in': _L1_attn_in['w_in'], 'L1_attn_b_in': _L1_attn_in['b_in'], 'L1_attn_w_out': _L1_attn_in['w_out'], 'L1_attn_b_out': _L1_attn_in['b_out'], 'L1_ffn_gate_w': _L1_ffn_in['gate_w'], 'L1_ffn_fc1_w': _L1_ffn_in['fc1_w'], 'L1_ffn_fc1_b': _L1_ffn_in['fc1_b'], 'L1_ffn_geglu_mult': _L1_ffn_in['geglu_mult'], 'L1_ffn_fc2_w': _L1_ffn_in['fc2_w'], 'L1_ffn_fc2_b': _L1_ffn_in['fc2_b'], 'L1_ffn_s_fc1_w': _L1_ffn_in['s_fc1_w'], 'L1_ffn_s_fc1_b': _L1_ffn_in['s_fc1_b'], 'L1_ffn_s_geglu_mult': _L1_ffn_in['s_geglu_mult'], 'L1_ffn_s_fc2_w': _L1_ffn_in['s_fc2_w'], 'L1_ffn_s_fc2_b': _L1_ffn_in['s_fc2_b']}
    _x0 = _d['L0_attn_x']
    _d['L0_attn_x'] = jax.random.normal(jax.random.fold_in(jax.random.key(seed), 1), (16, 256, 128), dtype=_x0.dtype)
    del _x0
    return _d

def reference(L0_attn_x, L0_attn_w_qkv, L0_attn_w_out, L0_ffn_gate_w, L0_ffn_gate_b, L0_ffn_w1, L0_ffn_b1, L0_ffn_w2, L0_ffn_b2, L1_attn_w_in, L1_attn_b_in, L1_attn_w_out, L1_attn_b_out, L1_ffn_gate_w, L1_ffn_fc1_w, L1_ffn_fc1_b, L1_ffn_geglu_mult, L1_ffn_fc2_w, L1_ffn_fc2_b, L1_ffn_s_fc1_w, L1_ffn_s_fc1_b, L1_ffn_s_geglu_mult, L1_ffn_s_fc2_w, L1_ffn_s_fc2_b):

    def _L0_attn_ref(x, w_qkv, w_out):
        import jax, jax.numpy as jnp
        import numpy as np
        N_HEADS = 16
        b, t, d = x.shape
        h = N_HEADS
        hd = d // h
        qkv = (x @ w_qkv).reshape(b, t, 3, h, hd)
        qkv = jnp.transpose(qkv, (2, 0, 3, 1, 4))
        q, k, v = (qkv[0], qkv[1], qkv[2])
        scale = 1.0 / jnp.sqrt(jnp.float32(hd))
        s = jnp.einsum('bhqd,bhkd->bhqk', q, k) * scale
        causal = jnp.tril(jnp.ones((t, t), dtype=bool))
        s = jnp.where(causal, s, -jnp.inf)
        p = jax.nn.softmax(s, axis=-1)
        o = jnp.einsum('bhqk,bhkd->bhqd', p, v)
        o = jnp.transpose(o, (0, 2, 1, 3)).reshape(b, t, d)
        return o @ w_out

    def _L0_ffn_ref(x, gate_w, gate_b, w1, b1, w2, b2):
        import jax, jax.numpy as jnp
        import numpy as np
        B, T, C = (4, 256, 128)
        E, H, K = (8, 256, 2)
        b, t, c = x.shape
        xf = x.reshape(b * t, c)
        logits = xf @ gate_w + gate_b
        probs = jax.nn.softmax(logits, axis=-1)
        gates, expert_idx = jax.lax.top_k(probs, K)
        h = jax.nn.relu(jnp.einsum('nc,ech->neh', xf, w1) + b1)
        expert_out = jnp.einsum('neh,ehc->nec', h, w2) + b2
        onehot = jax.nn.one_hot(expert_idx, E, dtype=xf.dtype)
        weights = jnp.einsum('nk,nke->ne', gates, onehot)
        out = jnp.einsum('ne,nec->nc', weights, expert_out)
        return out.reshape(b, t, c)

    def _L1_attn_ref(x, w_in, b_in, w_out, b_out):
        import jax, jax.numpy as jnp
        import numpy as np
        DIM = 128
        NUM_HEADS = 16
        HEAD_DIM = DIM // NUM_HEADS
        SCALE = HEAD_DIM ** (-0.5)
        B, N, C = x.shape
        H, D = (NUM_HEADS, HEAD_DIM)
        qkv = jnp.einsum('bnc,oc->bno', x, w_in) + b_in
        qkv = qkv.reshape(B, N, 3, H, D).transpose(2, 0, 3, 1, 4)
        q, k, v = (qkv[0], qkv[1], qkv[2])
        attn = jnp.einsum('bhnd,bhmd->bhnm', q, k) * SCALE
        attn = jax.nn.softmax(attn, axis=-1)
        out = jnp.einsum('bhnm,bhmd->bhnd', attn, v)
        out = out.transpose(0, 2, 1, 3).reshape(B, N, C)
        out = jnp.einsum('bnc,oc->bno', out, w_out) + b_out
        return out

    def _L1_ffn_ref(x, gate_w, fc1_w, fc1_b, geglu_mult, fc2_w, fc2_b, s_fc1_w, s_fc1_b, s_geglu_mult, s_fc2_w, s_fc2_b):
        import jax, jax.numpy as jnp
        import numpy as np
        S, B, D = (128, 2, 128)
        E, TOPK = (15, 3)
        F = 128
        FS = 256

        def _uinit(k, shape, out_dim):
            std = out_dim ** (-0.5)
            return jax.random.uniform(k, shape, jnp.float32, -std, std)
        s, b, d = x.shape
        xt = x.reshape(-1, d)
        T = xt.shape[0]
        logits = xt @ gate_w.T
        scores = jax.nn.softmax(logits, axis=-1)
        topk_w, topk_idx = jax.lax.top_k(scores, TOPK)
        topk_w = topk_w / (jnp.sum(topk_w, axis=-1, keepdims=True) + 1e-20)
        comb = jnp.zeros((T, E), xt.dtype).at[jnp.arange(T)[:, None], topk_idx].add(topk_w)
        h = jnp.einsum('td,efd->etf', xt, fc1_w) + fc1_b[:, None, :]
        xh, g = (h[..., :F], h[..., F:])
        a = jax.nn.gelu(g, approximate=False) * xh * geglu_mult[:, None, :]
        yexp = jnp.einsum('etf,edf->etd', a, fc2_w) + fc2_b[:, None, :]
        y = jnp.einsum('etd,te->td', yexp, comb)
        hs = xt @ s_fc1_w.T + s_fc1_b
        xs, gs = (hs[..., :FS], hs[..., FS:])
        as_ = jax.nn.gelu(gs, approximate=False) * xs * s_geglu_mult
        ys = as_ @ s_fc2_w.T + s_fc2_b
        return (y + ys).reshape(s, b, d)
    x = L0_attn_x
    x = _layernorm(x + _L0_attn_ref(x, L0_attn_w_qkv, L0_attn_w_out), axis=-1)
    x = _layernorm(x + _L0_ffn_ref(x, L0_ffn_gate_w, L0_ffn_gate_b, L0_ffn_w1, L0_ffn_b1, L0_ffn_w2, L0_ffn_b2), axis=-1)
    x = _layernorm(x + _L1_attn_ref(x, L1_attn_w_in, L1_attn_b_in, L1_attn_w_out, L1_attn_b_out), axis=-1)
    x = _layernorm(x + _L1_ffn_ref(x, L1_ffn_gate_w, L1_ffn_fc1_w, L1_ffn_fc1_b, L1_ffn_geglu_mult, L1_ffn_fc2_w, L1_ffn_fc2_b, L1_ffn_s_fc1_w, L1_ffn_s_fc1_b, L1_ffn_s_geglu_mult, L1_ffn_s_fc2_w, L1_ffn_s_fc2_b), axis=-1)
    return x

_drawn_inputs = setup_inputs


def setup_inputs(seed=0):
    import zlib

    import numpy as np

    out = dict(_drawn_inputs(seed))
    spreads = {'L0_ffn_gate_b': (0.0, 0.272),
     'L1_ffn_geglu_mult': (1.0, 0.6),
     'L1_ffn_s_geglu_mult': (1.0, 0.6)}
    factors = {'L0_attn_w_qkv': 5.711,
     'L0_attn_w_out': 5.607,
     'L0_ffn_b1': 7.649,
     'L0_ffn_b2': 4.314,
     'L1_attn_b_out': 2.759,
     'L1_ffn_fc1_b': 8.0,
     'L1_ffn_s_fc1_b': 8.0}
    for name, (base, spread) in spreads.items():
        noise = np.random.default_rng([zlib.crc32(name.encode()), seed]).standard_normal(out[name].shape)
        drawn = base * np.exp(spread * noise) if base else spread * noise
        out[name] = jnp.asarray(drawn.astype(out[name].dtype))
    for name, factor in factors.items():
        out[name] = (out[name] * factor).astype(out[name].dtype)
    return out
```

```python
from contextlib import ExitStack

import concourse.bass as bass
from concourse import mybir

F32 = mybir.dt.float32
F32R = mybir.dt.float32r
BF16 = mybir.dt.bfloat16
U32 = mybir.dt.uint32
ALU = mybir.AluOpType
ACT = mybir.ActivationFunctionType
AX = mybir.AxisListType

NB = 16
T = 256
D = 128
NH = 16
HD = D // NH
SCALE = float(HD) ** -0.5
E0, E1 = 8, 15
U1 = E1 + 2
EXPERTS = (E0, E1)
UNITS = (E0, U1)
EPS = 1e-5
NEG = -1e38
VW = HD + 1
RING = (4, 5)

C_B1 = 0
C_FC1 = C_B1 + 2 * E0
C_MULT = C_FC1 + 2 * U1
C_BQK = C_MULT + U1
NCOLS = C_BQK + 2
R_GB = 0
R_BV = R_GB + E0
R_BO = R_BV + D
NROWS = R_BO + D

PIECES = (0, 1, 2)
DMA = 16

K_A0PREP, K_A0, K_F0, K_A1PREP, K_A1, K_F1, K_OUT = -1, 0, 1, 1, 2, 3, 4
P2, P3 = 19.0, 38.5
FIRST, LAST = -1, NB - 1 + K_OUT
LOOP_FROM, LOOP_TO = 5, 15


def top_ops(L):
    return 17 if L == 0 else 24


def plan():
    s = []

    def add(at, name, L, k, x=0):
        s.append((at, len(s), name, L, k, x))

    def attention(at, L, k):
        for h in range(NH):
            add(at + h, "scores_T", L, k, h)
            add(at + h + 0.1, "exp", L, k, h)
            if h % 4 == 3:
                add(at + h + 2.05, "weigh_V", L, k, h // 4)
                add(at + h + 2.1, "keep_O", L, k, h // 4)

    def maxima(at, step, L, k):
        for h in range(NH):
            add(at + h * step, "scores", L, k, h)
            add(at + h * step + 0.05, "row_max", L, k, h)
        end = at + NH * step
        add(end + 0.3, "max_join", L, k)
        add(end + 0.5, "max_T", L, k)
        add(end + 0.6, "max_parts", L, k)
        add(end + 0.7, "max_rows", L, k)

    def prepare(at, L, k, gap):
        add(at, "x_T", 2 * L, k)
        add(at + 0.05, "x_T_keep", 2 * L, k)
        add(at + gap * 0.3, "x_T_split", 2 * L, k, 0)
        add(at + gap * 0.6, "x_T_split", 2 * L, k, 1)
        if L == 1:
            add(at + gap * 0.6, "residual_bias", L, k)
        add(at + gap * 1.0, "qk", L, k)
        add(at + gap * 1.05, "qk_keep", L, k)
        add(at + gap * 1.5, "v", L, k)
        for j in range(4):
            add(at + gap * (1.4 + 0.3 * j), "qk_part", L, k, j)
        add(at + gap * 1.9, "v_keep", L, k)
        add(at + gap * 2.4, "stack", L, k)

    def norm(at, site, k, gap):
        add(at, "sum", site, k)
        for blk in range(2):
            add(at + gap * (0.3 + 0.1 * blk), "stats", site, k, blk)
            add(at + gap * (0.6 + 0.1 * blk), "aggregate", site, k, blk)
        add(at + gap * 0.8, "inverse_std", site, k)
        for blk in range(2):
            add(at + gap * (1.9 + 0.1 * blk), "normalise", site, k, blk)

    def after_attention(at, L, k, gap):
        for blk in range(2):
            add(at + gap * blk, "O_T", L, k, blk)
            add(at + gap * (blk + 0.2), "O_inverse", L, k, blk)
            add(at + gap * (blk + 0.5), "O_norm", L, k, blk)
        add(at + gap * 2.0, "O_back", L, k)
        add(at + gap * 2.05, "O_back_keep", L, k)
        add(at + gap * 2.8, "out_proj", L, k)
        norm(at + gap * 2.9, 2 * L, k, gap)

    def gate(at, L, k, gap):
        add(at, "x_T", 2 * L + 1, k)
        add(at + 0.05, "x_T_keep", 2 * L + 1, k)
        add(at + gap * 0.3, "x_T_split", 2 * L + 1, k, 0)
        add(at + gap * 0.6, "x_T_split", 2 * L + 1, k, 1)
        add(at + gap * 0.9, "logits", L, k)
        for j in range(4):
            add(at + gap * (1.0 + 0.2 * j), "top", L, k, j)
        add(at + gap * 1.9, "gate_exp", L, k)
        n = top_ops(L)
        for j in range(4, n):
            add(at + gap * (2.3 + 2.7 * (j - 4) / (n - 4)), "top", L, k, j)
        add(at + gap * 5.1, "weights_T", L, k)
        add(at + gap * 5.15, "weights_T_keep", L, k)
        add(at + gap * 5.2, "weights_store", L, k)
        for e in range(RING[L]):
            add(at + gap * 5.3, "weights_load", L, k, e)

    def after_experts(at, L, k, gap):
        add(at, "y_keep", L, k)
        add(at + gap * 0.9, "y_T", L, k)
        norm(at + gap * 1.0, 2 * L + 1, k, gap)

    def experts(at, L, k, step, lag):
        for e in range(UNITS[L]):
            add(at + e * step, "fc1", L, k, e)
            add(at + e * step + 0.1, "activate", L, k, e)
            if L == 1:
                add(at + e * step + lag[0], "times", L, k, e)
            if e < EXPERTS[L]:
                add(at + e * step + lag[1], "weigh", L, k, e)
                if e + RING[L] < EXPERTS[L]:
                    add(at + e * step + lag[1] + 0.01, "weights_load", L, k, e + RING[L])
            add(at + e * step + lag[2], "act_hi", L, k, e)
            add(at + e * step + lag[3], "act_lo", L, k, e)
            add(at + e * step + lag[4], "fc2", L, k, e)
        add(at + (UNITS[L] - 1) * step + lag[4] + 0.01, "fc2_bias", L, k)

    after_experts(0.0, 1, K_OUT, 1.0)
    add(2.3, "store_out", 1, K_OUT)
    add(2.4, "load_x", 0, K_A0PREP)
    attention(0.0, 0, K_A0)
    experts(0.5, 0, K_F0, 1.9, (0, 0.2, 1.9, 2.2, 4.0))
    maxima(0.3, 1.0, 1, K_A1)
    gate(3.0, 1, K_F1, 1.4)
    attention(P2, 1, K_A1)
    prepare(P2 + 0.2, 0, K_A0PREP, 0.9)
    after_experts(P2 + 2.6, 0, K_F0, 0.9)
    after_attention(P2 + 3.6, 0, K_A0, 0.9)
    gate(P2 + 9.2, 0, K_A0, 1.2)
    maxima(P2 + 4.3, 0.8, 0, K_A0PREP)
    experts(P3, 1, K_F1, 1.0, (0.7, 0.8, 2.2, 2.9, 4.3))
    prepare(P3 + 1.3, 1, K_A1PREP, 1.8)
    after_attention(P3 + 7.2, 1, K_A1, 1.8)
    s.sort()
    return [x[2:] for x in s]


PLAN = plan()
BANKS = ("ST0", "ST1", "S", "O", "M", "H0", "H1", "Y")


def active(t, k):
    return 0 <= t - k < NB


class Batch:

    def __init__(self, reg, c):
        self.reg, self.c, self.p = reg, c, c % 2

    def after(self, back):
        return self.reg is not None or self.c >= back

    def exists(self):
        return self.reg is not None or 0 <= self.c < NB

    def row(self):
        return self.c if self.reg is None else self.reg * 2 + self.c


class Signal:

    def __init__(self, sem, per):
        self.sem, self.per = sem, per

    def at(self, b, n, back=0):
        if b.reg is None:
            return (b.c - back) * self.per + n
        return b.reg * (2 * self.per) + ((b.c - back) * self.per + n)


def run_slots(eng, step):
    for t in range(FIRST, LOOP_FROM):
        for name, L, k, x in PLAN:
            if active(t, k):
                step(name, L, Batch(None, t - k), x)
    with eng.Fori(0, (LOOP_TO - LOOP_FROM) // 2) as reg:
        for u in range(2):
            for name, L, k, x in PLAN:
                step(name, L, Batch(reg, LOOP_FROM + u - k), x)
    for t in range(LOOP_TO, LAST + 1):
        for name, L, k, x in PLAN:
            if active(t, k):
                step(name, L, Batch(None, t - k), x)


def build(nc, x_in, cols_in, rows_in, wqk0_in, wvo0_in, wqk1_in, wvo1_in, gw_in,
          w1_0_in, w2_0_in, w1_1_in, w2_1_in, b2_0_in, b2_1_in, ident_in, masks_in, out):
    ctx = ExitStack()
    with ctx:
        def sb(name, shape, dt=F32):
            return ctx.enter_context(nc.sbuf_tensor(name, shape, dt))

        def dram(name, shape, dt):
            return nc.dram_tensor(name, shape, dt, kind="Internal").ap()

        def signal(name, per=1):
            return Signal(ctx.enter_context(nc.semaphore(name)), per)

        def pair(name, per=1):
            return [signal(f"{name}{L}", per) for L in range(2)]

        wqk_hi = sb("wqk_hi", [D, 2, 2 * D], F32R)
        wqk_lo = sb("wqk_lo", [D, 2, 2 * D], F32R)
        wvo = sb("wvo", [D, 2, 2, D])
        gw = sb("gw", [D, E0 + E1])
        w1_hi = [sb("w1_hi0", [D, E0, 2, D], F32R), sb("w1_hi1", [D, U1, 2, D], F32R)]
        w1_lo = [sb("w1_lo0", [D, E0, 2, D], F32R), sb("w1_lo1", [D, U1, 2, D], F32R)]
        w2_hi = [sb("w2_hi0", [D, E0, 2, D], F32R), sb("w2_hi1", [D, U1, 1, D], F32R)]
        w2_lo = [sb("w2_lo0", [D, E0, 2, D], F32R), sb("w2_lo1", [D, U1, 1, D], F32R)]
        b2 = sb("b2", [D, 2, D])
        cols = sb("cols", [D, NCOLS])
        rows = sb("rows", [D, NROWS])
        ident = sb("ident", [D, D])
        identb = sb("identb", [D, D], BF16)
        masks = sb("masks", [D, 2, D], BF16)
        iota = sb("iota", [D, E1])
        minus_half = sb("minus_half", [D, 2])
        eps = sb("eps", [D, 2])
        Qs = [sb(f"Qs{L}", [D, NH, T], BF16) for L in range(2)]
        Ks = [sb(f"Ks{L}", [D, NH, T], BF16) for L in range(2)]
        V = [sb(f"V{L}", [D, 2, NH * VW + 32 - VW]) for L in range(2)]
        P = sb("P", [D, 2, 4, 2 * T])
        OT = sb("OT", [D, 4, T])
        On = sb("On", [D, 2, D])
        OnT = sb("OnT", [D, T])
        xT = sb("xT", [D, T])
        xTh = [sb(f"xTh{s}", [D, T], F32R) for s in range(3)]
        xTl = [sb(f"xTl{s}", [D, T], F32R) for s in range(3)]
        u = sb("u", [D, 2 * T])
        parts = sb("parts", [D, 3, 2 * T], BF16)
        mp = [sb("mp0", [D, 3, NH]), sb("mp1", [D, 2, NH])]
        mrow = sb("mrow", [NH, 2, T], BF16)
        oinv = sb("oinv", [D, 2, NH])
        xa = [[sb(f"xa{L}{p}", [D, 2, D]) for p in range(2)] for L in range(2)]
        xb = [[sb(f"xb{L}{p}", [D, 2, D]) for p in range(2)] for L in range(2)]
        xo = sb("xo", [D, 2, D])
        st6 = sb("st6", [D, 4, 2, 6])
        mv = sb("mv", [D, 4, 2, 2])
        rstd = sb("rstd", [D, 4, 2])
        lg = [sb(f"lg{L}", [D, 2, EXPERTS[L]]) for L in range(2)]
        pe_ = [sb(f"pe{L}", [D, 2, EXPERTS[L]]) for L in range(2)]
        mk = [sb(f"mk{L}", [D, 2, EXPERTS[L]]) for L in range(2)]
        m8 = [sb(f"m8{L}", [D, 2, 8]) for L in range(2)]
        ix = [sb(f"ix{L}", [D, 2, 8], U32) for L in range(2)]
        ixf = [sb(f"ixf{L}", [D, 2, 8]) for L in range(2)]
        gs = [sb(f"gs{L}", [D, 4, 2]) for L in range(2)]
        comb = [sb(f"comb{L}", [D, 2, D]) for L in range(2)]
        combT = [sb(f"combT{L}", [D, T]) for L in range(2)]
        cw = [sb(f"cw{L}", [D, RING[L], T]) for L in range(2)]
        R = sb("R", [D, 6, T])
        Ah = sb("Ah", [D, 6, T], F32R)
        Al = sb("Al", [D, 6, T], F32R)
        yT = sb("yT", [D, T])
        ge = P[:, 0, :, :].rearrange("p a b -> p (a b)")

        qk_d = [dram(f"qk_d{L}", (2, 3, HD, NH, T), BF16) for L in range(2)]
        m_d = [dram(f"m_d{L}", (2, NH, T), BF16) for L in range(2)]
        cw_d = [dram(f"cw_d{L}", (EXPERTS[L], T), F32) for L in range(2)]

        bank = {n: ctx.enter_context(nc.psum_tensor(f"bank_{n}", [D, 512], F32)) for n in BANKS}

        w_in = signal("w_in")
        wst_in = [signal(f"wst_in{i}") for i in range(2)]
        w_scaled = signal("w_scaled")
        w_hi_done = signal("w_hi_done")
        w_lo_done = signal("w_lo_done")
        const_dve = signal("const_dve")
        const_pool = signal("const_pool")
        wait_taken = [signal("wait_taken_sp"), signal("wait_taken_dve")]
        dve_engine = nc.vector
        x_loaded = [signal(f"x_loaded{p}", DMA) for p in range(2)]
        out_stored = signal("out_stored", DMA)
        xT_ps = [signal(f"xT_ps{s}") for s in range(4)]
        xT_kept = [signal(f"xT_kept{s}") for s in range(4)]
        xT_split = [signal(f"xT_split{s}", 2) for s in range(4)]
        bias_added = signal("bias_added")
        qk_ps = pair("qk_ps")
        qk_kept = [signal("qk_kept0", 1), signal("qk_kept1", 2)]
        qk_parts = pair("qk_parts", 4)
        qk_written = pair("qk_written", 6 * DMA)
        stacked = pair("stacked", 6 * DMA)
        v_ps = pair("v_ps")
        v_kept = pair("v_kept")
        s_ps = pair("s_ps", NH)
        maxed = [signal("maxed0", NH + 1), signal("maxed1", NH)]
        mT_ps = pair("mT_ps")
        m_parts = pair("m_parts", 2)
        m_written = pair("m_written", DMA)
        m_stacked = pair("m_stacked", DMA)
        st_ps = pair("st_ps", NH)
        exped = pair("exped", NH)
        o_ps = pair("o_ps", 4)
        o_kept = pair("o_kept", 4)
        oT_ps = pair("oT_ps", 2)
        o_norm = pair("o_norm", 4)
        onT_ps = pair("onT_ps")
        onT_kept = pair("onT_kept")
        proj_ps = pair("proj_ps")
        ln = [signal(f"ln{s}", 7) for s in range(4)]
        ln_pool = [signal(f"ln_pool{s}", 2) for s in range(4)]
        lg_ps = pair("lg_ps")
        top = [signal(f"top{L}", top_ops(L)) for L in range(2)]
        gexp = pair("gexp", 2)
        cT_ps = pair("cT_ps")
        cT_kept = pair("cT_kept")
        cw_stored = pair("cw_stored", DMA)
        cw_loaded = [[signal(f"cw_loaded{L}{i}", EXPERTS[L] // RING[L] * DMA) for i in range(RING[L])]
                     for L in range(2)]
        h_ps = [signal(f"h_ps{L}", UNITS[L]) for L in range(2)]
        acted = [signal("acted0", 2 * E0), signal("acted1", U1)]
        timed = signal("timed", U1)
        weighed = [signal(f"weighed{L}", EXPERTS[L]) for L in range(2)]
        hi_done = [signal(f"hi_done{L}", UNITS[L]) for L in range(2)]
        lo_done = [signal(f"lo_done{L}", UNITS[L]) for L in range(2)]
        fc2_ps = [signal(f"fc2_ps{L}", UNITS[L]) for L in range(2)]
        y_ps = pair("y_ps")
        y_kept = pair("y_kept")
        yT_ps = pair("yT_ps")

        def take_wait(eng):
            eng.sem_inc(wait_taken[int(eng is dve_engine)].sem, 1)

        def stage_in(s):
            return (xa[0], xb[0], xa[1], xb[1])[s]

        def norm_out(site):
            return (xb[0], xa[1], xb[1], (xo, xo))[site]

        def wait_stage_in(eng, s, b):
            if s == 0:
                wait_x(eng, b)
            else:
                eng.wait_ge(ln[s - 1].sem, ln[s - 1].at(b, 7))

        def wait_x(eng, b):
            if b.reg is None:
                eng.wait_ge(x_loaded[b.p].sem, (b.c // 2 + 1) * DMA)
            else:
                eng.wait_ge(x_loaded[b.p].sem, b.reg * DMA + (b.c // 2 + 1) * DMA)

        def split_of(s):
            return 0 if s % 2 == 0 else (1 if s == 1 else 2)

        flat = lambda w: w[:, :, :, :].rearrange("p a b c -> p (a b c)")
        weight_pieces = []
        for L, src in ((0, wqk0_in), (1, wqk1_in)):
            weight_pieces.append((src, 0, 2 * D, wqk_hi[:, L, :], wqk_lo[:, L, :], False))
        for src, hi, lo, mult in ((w1_0_in, w1_hi[0], w1_lo[0], False), (w2_0_in, w2_hi[0], w2_lo[0], False),
                                  (w1_1_in, w1_hi[1], w1_lo[1], False), (w2_1_in, w2_hi[1], w2_lo[1], True)):
            n = src.shape[1]
            for a in range(0, n, 2048):
                z = min(n, a + 2048)
                weight_pieces.append((src, a, z, flat(hi)[:, a:z], flat(lo)[:, a:z], mult))
        stage = [P[:, i, :, :].rearrange("p a b -> p (a b)") for i in range(2)]
        scaled_before = [sum(m for *_, m in weight_pieces[:i + 1]) for i in range(len(weight_pieces))]
        NPIECES = len(weight_pieces)
        SMALL_LOADS = 9

        def ones_of_V(L, blk):
            return V[L][:, blk, 0:NH * VW].rearrange("p (h w) -> p h w", w=VW)[:, :, HD:VW]

        CONSTANTS = [(b2[:, :, :], 0.0), (minus_half[:, :], -0.5), (eps[:, :], EPS)]
        for L in range(2):
            CONSTANTS += [(comb[L][:, :, :], 0.0), (V[L][:, :, :], 0.0), (Qs[L][:, :, :], 0.0),
                          (Ks[L][0:96, :, :], 0.0), (Ks[L][96:128, :, :], 1.0)]
            CONSTANTS += [(ones_of_V(L, blk), 1.0) for blk in range(2)]
        CONSTANTS += [(comb[1][:, :, E1:E1 + 1], 1.0)]
        CONSTANTS += [(iota[:, e:e + 1], float(e)) for e in range(E1)]

        block = ctx.enter_context(nc.Block())

        @block.sync
        def _(sp):
            for dst, src in ((cols[:, :], cols_in), (rows[:, :], rows_in.partition_broadcast(D)),
                             (ident[:, :], ident_in), (masks[:, :, :].rearrange("p a b -> p (a b)"), masks_in),
                             (gw[:, :], gw_in),
                             (wvo[:, 0, :, :].rearrange("p a b -> p (a b)"), wvo0_in),
                             (wvo[:, 1, :, :].rearrange("p a b -> p (a b)"), wvo1_in)):
                sp.dma_start(dst, src).then_inc(w_in.sem, DMA)
            sp.wait_ge(const_pool.sem, 1)
            sp.dma_start(b2[0:E0, 0, :], b2_0_in).then_inc(w_in.sem, DMA)
            sp.dma_start(b2[0:E1 + 1, 1, :], b2_1_in).then_inc(w_in.sem, DMA)
            for i, (src, a, z, _, _, _) in enumerate(weight_pieces):
                if i >= 2:
                    sp.wait_ge(w_lo_done.sem, i - 1)
                sp.dma_start(stage[i % 2][:, 0:z - a], src[:, a:z]).then_inc(wst_in[i % 2].sem, DMA)

            def load_x(b):
                if b.after(2):
                    sp.wait_ge(xT_ps[0].sem, xT_ps[0].at(b, 1, back=2))
                take_wait(sp)
                if b.after(2):
                    sp.wait_ge(ln[0].sem, ln[0].at(b, 1, back=2))
                take_wait(sp)
                r = b.row()
                src = x_in[r:r + 1] if b.reg is None else x_in[bass.ds(r, 1)]
                sp.dma_start(xa[0][b.p][:, :, :],
                             src.rearrange("o (c p) d -> p (o c) d", p=D)).then_inc(x_loaded[b.p].sem, DMA)

            def stack(L, b):
                sp.wait_ge(qk_parts[L].sem, qk_parts[L].at(b, 4))
                take_wait(sp)
                if b.after(1):
                    sp.wait_ge(stacked[L].sem, stacked[L].at(b, 6 * DMA, back=1))
                take_wait(sp)
                for i in PIECES:
                    for side in range(2):
                        sp.dma_start(qk_d[L][side, i].rearrange("d h t -> h d t"),
                                     parts[:, i, side * T:(side + 1) * T]).then_inc(qk_written[L].sem, DMA)
                sp.wait_ge(qk_written[L].sem, qk_written[L].at(b, 6 * DMA))
                take_wait(sp)
                sp.wait_ge(const_pool.sem, len(CONSTANTS))
                if b.after(1):
                    sp.wait_ge(st_ps[L].sem, st_ps[L].at(b, NH, back=1))
                take_wait(sp)
                for i in PIECES:
                    rows_ = slice(24 * i, 24 * i + 24)
                    q_src = qk_d[L][0, i].rearrange("d h t -> d (h t)").unsqueeze(0).broadcast_to((3, HD, NH * T))
                    k_src = qk_d[L][1].rearrange("i d h t -> (i d) (h t)")
                    sp.dma_start(Qs[L][rows_, :, :].rearrange("p h t -> p (h t)"), q_src)\
                        .then_inc(stacked[L].sem, DMA)
                    sp.dma_start(Ks[L][rows_, :, :].rearrange("p h t -> p (h t)"), k_src)\
                        .then_inc(stacked[L].sem, DMA)

            def max_rows(L, b):
                sp.wait_ge(m_parts[L].sem, m_parts[L].at(b, 2))
                take_wait(sp)
                if b.after(1):
                    sp.wait_ge(m_stacked[L].sem, m_stacked[L].at(b, DMA, back=1))
                sp.dma_start(m_d[L].rearrange("i h t -> h i t"), mrow[:, :, :]).then_inc(m_written[L].sem, DMA)
                sp.wait_ge(m_written[L].sem, m_written[L].at(b, DMA))
                sp.dma_start(Qs[L][96:98, :, :].rearrange("p h t -> p (h t)"),
                             m_d[L].rearrange("i h t -> i (h t)")).then_inc(m_stacked[L].sem, DMA)

            def weights_store(L, b):
                sp.wait_ge(cT_kept[L].sem, cT_kept[L].at(b, 1))
                take_wait(sp)
                for i in range(RING[L]):
                    if b.after(1):
                        sp.wait_ge(cw_loaded[L][i].sem, cw_loaded[L][i].at(b, cw_loaded[L][i].per, back=1))
                sp.dma_start(cw_d[L], combT[L][0:EXPERTS[L], :]).then_inc(cw_stored[L].sem, DMA)
                sp.wait_ge(cw_stored[L].sem, cw_stored[L].at(b, DMA))
                take_wait(sp)

            def weights_load(L, b, e):
                if e < RING[L]:
                    if b.after(1):
                        sp.wait_ge(weighed[L].sem, weighed[L].at(b, EXPERTS[L] - RING[L] + e + 1, back=1))
                else:
                    sp.wait_ge(weighed[L].sem, weighed[L].at(b, e - RING[L] + 1))
                sp.dma_start(cw[L][:, e % RING[L], :], cw_d[L][e].partition_broadcast(D))\
                    .then_inc(cw_loaded[L][e % RING[L]].sem, DMA)

            def store_out(b):
                sp.wait_ge(ln[3].sem, ln[3].at(b, 7))
                take_wait(sp)
                r = b.row()
                dst = out[r:r + 1] if b.reg is None else out[bass.ds(r, 1)]
                sp.dma_start(dst.rearrange("o (c p) d -> p (o c) d", p=D), xo[:, :, :])\
                    .then_inc(out_stored.sem, DMA)

            def step(name, L, b, x):
                if name == "load_x":
                    load_x(b)
                if name == "stack":
                    stack(L, b)
                if name == "max_rows":
                    max_rows(L, b)
                if name == "weights_store":
                    weights_store(L, b)
                if name == "weights_load":
                    weights_load(L, b, x)
                if name == "store_out":
                    store_out(b)

            run_slots(sp, step)
            sp.wait_ge(out_stored.sem, NB * DMA)

        @block.gpsimd
        def _(pool):
            for n, (tile, value) in enumerate(CONSTANTS):
                if n:
                    pool.wait_ge(const_pool.sem, n)
                pool.memset(tile, value).then_inc(const_pool.sem, 1)
            pool.wait_ge(const_pool.sem, len(CONSTANTS))

            def inverse_std(site, b):
                pool.wait_ge(ln[site].sem, ln[site].at(b, 5))
                if b.after(1):
                    pool.wait_ge(ln[site].sem, ln[site].at(b, 7, back=1))
                pool.tensor_tensor(rstd[:, site, :], mv[:, site, :, 1], eps[:, :], ALU.add)\
                    .then_inc(ln_pool[site].sem, 1)
                pool.wait_ge(ln_pool[site].sem, ln_pool[site].at(b, 1))
                pool.tensor_tensor(rstd[:, site, :], rstd[:, site, :], minus_half[:, :], ALU.pow)\
                    .then_inc(ln_pool[site].sem, 1)

            def residual_bias(b):
                pool.wait_ge(xT_ps[2].sem, xT_ps[2].at(b, 1))
                pool.wait_ge(w_in.sem, SMALL_LOADS * DMA)
                pool.tensor_tensor(xa[1][b.p][:, :, :], xa[1][b.p][:, :, :],
                                   rows[:, R_BO:R_BO + D].unsqueeze(1).broadcast_to((D, 2, D)), ALU.add)\
                    .then_inc(bias_added.sem, 1)

            def weigh(L, b, e):
                w = cw[L][:, e % RING[L], :]
                turn = (e // RING[L] + 1) * DMA
                pool.wait_ge(cw_loaded[L][e % RING[L]].sem, cw_loaded[L][e % RING[L]].at(b, turn))
                if L == 0:
                    pool.wait_ge(acted[0].sem, acted[0].at(b, 2 * e + 2))
                    a = R[:, 2 * (e % 3):2 * (e % 3) + 2, :]
                    w = w.unsqueeze(1).broadcast_to((D, 2, T))
                else:
                    pool.wait_ge(timed.sem, timed.at(b, e + 1))
                    a = R[:, e % 6, :]
                pool.tensor_tensor(a, a, w, ALU.mult).then_inc(weighed[L].sem, 1)

            def step(name, L, b, x):
                if name == "inverse_std":
                    inverse_std(L, b)
                if name == "residual_bias":
                    residual_bias(b)
                if name == "weigh":
                    weigh(L, b, x)

            run_slots(pool, step)

        @block.scalar
        def _(act):
            act.wait_ge(w_in.sem, SMALL_LOADS * DMA)
            for i, (_, a, z, hi, _, mult) in enumerate(weight_pieces):
                act.wait_ge(wst_in[i % 2].sem, (i // 2 + 1) * DMA)
                if mult:
                    act.wait_ge(w_scaled.sem, scaled_before[i])
                act.activation(hi, stage[i % 2][:, 0:z - a], ACT.Copy).then_inc(w_hi_done.sem, 1)

            def x_T_keep(s, b):
                act.wait_ge(xT_ps[s].sem, xT_ps[s].at(b, 1))
                before = Batch(b.reg, b.c + (K_A0PREP - K_F1, K_A0 - K_A0PREP, K_A1PREP - K_A0,
                                             K_F1 - 1 - K_A1PREP)[s])
                if before.exists():
                    user = (lg_ps[1], v_ps[0], lg_ps[0], v_ps[1])[s]
                    act.wait_ge(user.sem, user.at(before, 1))
                act.activation(xT[:, :], bank["M"][:, 0:T], ACT.Copy).then_inc(xT_kept[s].sem, 1)

            def qk_keep(L, b):
                act.wait_ge(qk_ps[L].sem, qk_ps[L].at(b, 1))
                if L == 0:
                    act.activation(u[:, :], bank["M"][:, :], ACT.Copy).then_inc(qk_kept[0].sem, 1)
                    act.wait_ge(qk_kept[0].sem, qk_kept[0].at(b, 1))
                else:
                    for side in range(2):
                        act.activation(u[:, side * T:(side + 1) * T], bank["M"][:, side * T:(side + 1) * T],
                                       ACT.Identity, bias=cols[:, C_BQK + side:C_BQK + side + 1])\
                            .then_inc(qk_kept[1].sem, 1)

            def exp(L, b, h):
                act.wait_ge(st_ps[L].sem, st_ps[L].at(b, h + 1))
                n = 2 * T if L == 1 else 3 * D
                act.activation(P[:, (h // 4) % 2, h % 4, 0:n], bank[("ST0", "ST1")[h % 2]][:, 0:n], ACT.Exp,
                               scale=SCALE).then_inc(exped[L].sem, 1)

            def O_back_keep(L, b):
                act.wait_ge(onT_ps[L].sem, onT_ps[L].at(b, 1))
                act.activation(OnT[:, :], bank["M"][:, 0:T], ACT.Copy).then_inc(onT_kept[L].sem, 1)

            def gate_exp(L, b):
                act.wait_ge(top[L].sem, top[L].at(b, 4))
                if b.after(1):
                    act.wait_ge(top[L].sem, top[L].at(b, top_ops(L), back=1))
                for blk in range(2):
                    act.activation(pe_[L][:, blk, :], lg[L][:, blk, :], ACT.Exp, bias=gs[L][:, 0, blk:blk + 1],
                                   accum_out=gs[L][:, 1, blk:blk + 1]).then_inc(gexp[L].sem, 1)

            def weights_T_keep(L, b):
                act.wait_ge(cT_ps[L].sem, cT_ps[L].at(b, 1))
                if b.after(1):
                    act.wait_ge(y_ps[L].sem, y_ps[L].at(b, 1, back=1))
                if b.after(1):
                    act.wait_ge(cw_stored[L].sem, cw_stored[L].at(b, DMA, back=1))
                act.activation(combT[L][:, :], bank["M"][:, 0:T], ACT.Copy).then_inc(cT_kept[L].sem, 1)

            def activate(L, b, e):
                act.wait_ge(h_ps[L].sem, h_ps[L].at(b, e + 1))
                if L == 0:
                    if e >= 3:
                        act.wait_ge(lo_done[0].sem, lo_done[0].at(b, e - 2))
                    H = bank[("H0", "H1")[e % 2]]
                    for c in range(2):
                        act.activation(R[:, 2 * (e % 3) + c, :], H[:, c * T:(c + 1) * T], ACT.Relu,
                                       bias=cols[:, C_B1 + 2 * e + c:C_B1 + 2 * e + c + 1])\
                            .then_inc(acted[0].sem, 1)
                else:
                    if e >= 4:
                        act.wait_ge(timed.sem, timed.at(b, e - 3))
                    H = bank[("H0", "H1", "ST0", "ST1")[e % 4]]
                    act.activation(ge[:, (e % 4) * T:(e % 4 + 1) * T], H[:, T:2 * T], ACT.Gelu,
                                   bias=cols[:, C_FC1 + 2 * e + 1:C_FC1 + 2 * e + 2]).then_inc(acted[1].sem, 1)

            def act_hi(L, b, e):
                if e < EXPERTS[L]:
                    act.wait_ge(weighed[L].sem, weighed[L].at(b, e + 1))
                else:
                    act.wait_ge(timed.sem, timed.at(b, e + 1))
                depth = (3, 6)[L]
                if e >= depth:
                    act.wait_ge(fc2_ps[L].sem, fc2_ps[L].at(b, e - depth + 1))
                s = slice(2 * (e % 3), 2 * (e % 3) + 2) if L == 0 else slice(e % 6, e % 6 + 1)
                act.activation(Ah[:, s, :], R[:, s, :], ACT.Copy).then_inc(hi_done[L].sem, 1)

            def y_keep(L, b):
                act.wait_ge(y_ps[L].sem, y_ps[L].at(b, 1))
                act.activation(yT[:, :], bank["Y"][:, 0:T], ACT.Copy).then_inc(y_kept[L].sem, 1)

            def step(name, L, b, x):
                if name == "x_T_keep":
                    x_T_keep(L, b)
                if name == "qk_keep":
                    qk_keep(L, b)
                if name == "exp":
                    exp(L, b, x)
                if name == "O_back_keep":
                    O_back_keep(L, b)
                if name == "gate_exp":
                    gate_exp(L, b)
                if name == "weights_T_keep":
                    weights_T_keep(L, b)
                if name == "activate":
                    activate(L, b, x)
                if name == "act_hi":
                    act_hi(L, b, x)
                if name == "y_keep":
                    y_keep(L, b)

            run_slots(act, step)

        @block.tensor
        def _(pe):
            pe.wait_ge(const_pool.sem, len(CONSTANTS))
            pe.wait_ge(w_in.sem, SMALL_LOADS * DMA)
            pe.wait_ge(const_dve.sem, 1)
            pe.wait_ge(w_hi_done.sem, NPIECES)
            pe.wait_ge(w_lo_done.sem, NPIECES)

            def product3(o, w_hi, w_lo, a_hi, a_lo, start, stop):
                nc.tensor.matmul(o, w_hi, a_hi, start=start, stop=False, skip_group_check=True)
                nc.tensor.matmul(o, w_lo, a_hi, start=False, stop=False, skip_group_check=True)
                return nc.tensor.matmul(o, w_hi, a_lo, start=False, stop=stop, skip_group_check=True)

            M = bank["M"]

            filled = {}

            def x_T(s, b):
                if "M" in filled:
                    sig, before, n_read = filled["M"]
                    pe.wait_ge(sig.sem, sig.at(before, n_read))
                filled["M"] = (xT_kept[s], b, 1)
                wait_stage_in(pe, s, b)
                for blk in range(2):
                    m = pe.transpose(M[:, blk * D:(blk + 1) * D], stage_in(s)[b.p][:, blk, :], ident[:, :])
                m.then_inc(xT_ps[s].sem, 1)

            def qk(L, b):
                if "M" in filled:
                    sig, before, n_read = filled["M"]
                    pe.wait_ge(sig.sem, sig.at(before, n_read))
                filled["M"] = (qk_kept[L], b, qk_kept[L].per)
                pe.wait_ge(xT_split[2 * L].sem, xT_split[2 * L].at(b, 2))
                for side in range(2):
                    w = slice(side * D, (side + 1) * D)
                    m = product3(M[:, side * T:(side + 1) * T], wqk_hi[:, L, w], wqk_lo[:, L, w],
                                 xTh[0][:, :], xTl[0][:, :], True, True)
                m.then_inc(qk_ps[L].sem, 1)

            def v(L, b):
                if "M" in filled:
                    sig, before, n_read = filled["M"]
                    pe.wait_ge(sig.sem, sig.at(before, n_read))
                filled["M"] = (v_kept[L], b, 1)
                pe.wait_ge(xT_kept[2 * L].sem, xT_kept[2 * L].at(b, 1))
                for blk in range(2):
                    m = pe.matmul(M[:, blk * D:(blk + 1) * D], xT[:, blk * D:(blk + 1) * D], wvo[:, L, 0, :])
                m.then_inc(v_ps[L].sem, 1)

            def scores(L, b, h):
                k = ("S", "H0", "H1")[h % 3] if L == 0 else "S"
                S = bank[k]
                if k in filled:
                    sig, before, n_read = filled[k]
                    pe.wait_ge(sig.sem, sig.at(before, n_read))
                filled[k] = (maxed[L], b, h + 1)
                if h == 0:
                    pe.wait_ge(stacked[L].sem, stacked[L].at(b, 6 * DMA))
                if L == 1:
                    for qb in range(2):
                        m = pe.matmul(S[:, qb * T:(qb + 1) * T], Qs[1][0:96, h, qb * D:(qb + 1) * D],
                                      Ks[1][0:96, h, :])
                else:
                    for qb, (o, n) in enumerate(((0, D), (D, 2 * D))):
                        pe.matmul(S[:, o:o + n], Qs[0][0:96, h, qb * D:(qb + 1) * D], Ks[0][0:96, h, 0:n],
                                  start=True, stop=False, skip_group_check=True)
                        m = pe.matmul(S[:, o + n - D:o + n], identb[:, :], masks[:, 0, :],
                                      start=False, stop=True, skip_group_check=True)
                m.then_inc(s_ps[L].sem, 1)

            def max_T(L, b):
                if "M" in filled:
                    sig, before, n_read = filled["M"]
                    pe.wait_ge(sig.sem, sig.at(before, n_read))
                filled["M"] = (m_parts[L], b, 2)
                pe.wait_ge(maxed[L].sem, maxed[L].at(b, maxed[L].per))
                for qb in range(2):
                    m = pe.transpose(M[0:NH, qb * D:(qb + 1) * D], mp[L][:, qb, :], ident[:, :])
                m.then_inc(mT_ps[L].sem, 1)

            def scores_T(L, b, h):
                k = ("ST0", "ST1")[h % 2]
                S = bank[k]
                if k in filled:
                    sig, before, n_read = filled[k]
                    pe.wait_ge(sig.sem, sig.at(before, n_read))
                filled[k] = (exped[L], b, h + 1)
                if h == 0:
                    pe.wait_ge(m_stacked[L].sem, m_stacked[L].at(b, DMA))
                if L == 1:
                    for kb in range(2):
                        m = pe.matmul(S[:, kb * T:(kb + 1) * T], Ks[1][:, h, kb * D:(kb + 1) * D], Qs[1][:, h, :])
                else:
                    for kb, (o, n) in enumerate(((0, 2 * D), (2 * D, D))):
                        pe.matmul(S[:, o:o + n], Ks[0][:, h, kb * D:(kb + 1) * D], Qs[0][:, h, kb * D:T],
                                  start=True, stop=False, skip_group_check=True)
                        m = pe.matmul(S[:, o:o + D], identb[:, :], masks[:, 1, :],
                                      start=False, stop=True, skip_group_check=True)
                m.then_inc(st_ps[L].sem, 1)

            def weigh_V(L, b, g):
                if "O" in filled:
                    sig, before, n_read = filled["O"]
                    pe.wait_ge(sig.sem, sig.at(before, n_read))
                filled["O"] = (o_kept[L], b, g + 1)
                pe.wait_ge(exped[L].sem, exped[L].at(b, 4 * g + 4))
                if g == 0:
                    pe.wait_ge(v_kept[L].sem, v_kept[L].at(b, 1))
                O = bank["O"]
                for kb in range(2):
                    for j in range(4):
                        h = 4 * g + j
                        w = V[L][:, kb, h * VW:h * VW + 32]
                        if L == 1 or kb == 0:
                            o, a = O[32 * j:32 * j + 32, 0:T], P[:, g % 2, j, kb * T:(kb + 1) * T]
                        else:
                            o, a = O[32 * j:32 * j + 32, D:T], P[:, g % 2, j, T:T + D]
                        m = pe.matmul(o, w, a, start=(kb == 0), stop=(kb == 1), skip_group_check=True)
                m.then_inc(o_ps[L].sem, 1)

            def O_T(L, b, blk):
                if "M" in filled:
                    sig, before, n_read = filled["M"]
                    pe.wait_ge(sig.sem, sig.at(before, n_read))
                filled["M"] = (o_norm[L], b, 2 * blk + 2)
                if blk == 0:
                    pe.wait_ge(o_kept[L].sem, o_kept[L].at(b, 4))
                for g in range(4):
                    m = pe.transpose(M[:, g * D:(g + 1) * D], OT[:, g, blk * D:(blk + 1) * D], ident[:, :])
                m.then_inc(oT_ps[L].sem, 1)

            def O_back(L, b):
                if "M" in filled:
                    sig, before, n_read = filled["M"]
                    pe.wait_ge(sig.sem, sig.at(before, n_read))
                filled["M"] = (onT_kept[L], b, 1)
                pe.wait_ge(o_norm[L].sem, o_norm[L].at(b, 4))
                for blk in range(2):
                    m = pe.transpose(M[:, blk * D:(blk + 1) * D], On[:, blk, :], ident[:, :])
                m.then_inc(onT_ps[L].sem, 1)

            def out_proj(L, b):
                if "M" in filled:
                    sig, before, n_read = filled["M"]
                    pe.wait_ge(sig.sem, sig.at(before, n_read))
                filled["M"] = (ln[2 * L], b, 1)
                pe.wait_ge(onT_kept[L].sem, onT_kept[L].at(b, 1))
                for blk in range(2):
                    m = pe.matmul(M[:, blk * D:(blk + 1) * D], OnT[:, blk * D:(blk + 1) * D], wvo[:, L, 1, :])
                m.then_inc(proj_ps[L].sem, 1)

            def logits(L, b):
                if "M" in filled:
                    sig, before, n_read = filled["M"]
                    pe.wait_ge(sig.sem, sig.at(before, n_read))
                filled["M"] = (top[L], b, 1)
                pe.wait_ge(xT_kept[2 * L + 1].sem, xT_kept[2 * L + 1].at(b, 1))
                n = EXPERTS[L]
                w = gw[:, 0:E0] if L == 0 else gw[:, E0:E0 + E1]
                for blk in range(2):
                    m = pe.matmul(M[:, blk * n:(blk + 1) * n], xT[:, blk * D:(blk + 1) * D], w)
                m.then_inc(lg_ps[L].sem, 1)

            def weights_T(L, b):
                if "M" in filled:
                    sig, before, n_read = filled["M"]
                    pe.wait_ge(sig.sem, sig.at(before, n_read))
                filled["M"] = (cT_kept[L], b, 1)
                pe.wait_ge(top[L].sem, top[L].at(b, top_ops(L)))
                for blk in range(2):
                    m = pe.transpose(M[:, blk * D:(blk + 1) * D], comb[L][:, blk, :], ident[:, :])
                m.then_inc(cT_ps[L].sem, 1)

            def fc1(L, b, e):
                k = ("H0", "H1")[e % 2] if L == 0 else ("H0", "H1", "ST0", "ST1")[e % 4]
                H = bank[k]
                if k in filled:
                    sig, before, n_read = filled[k]
                    pe.wait_ge(sig.sem, sig.at(before, n_read))
                filled[k] = ((acted[0], timed)[L], b, (2 - L) * (e + 1))
                if e == 0:
                    pe.wait_ge(xT_split[2 * L + 1].sem, xT_split[2 * L + 1].at(b, 2))
                for c in range(2):
                    m = product3(H[:, c * T:(c + 1) * T], w1_hi[L][:, e, c, :], w1_lo[L][:, e, c, :],
                                 xTh[1 + L][:, :], xTl[1 + L][:, :], True, True)
                m.then_inc(h_ps[L].sem, 1)

            def fc2(L, b, e):
                if e == 0:
                    if "Y" in filled:
                        sig, before, n_read = filled["Y"]
                        pe.wait_ge(sig.sem, sig.at(before, n_read))
                    filled["Y"] = (y_kept[L], b, 1)
                pe.wait_ge(lo_done[L].sem, lo_done[L].at(b, e + 1))
                pe.wait_ge(hi_done[L].sem, hi_done[L].at(b, e + 1))
                for c in range(2 - L):
                    s = 2 * (e % 3) + c if L == 0 else e % 6
                    m = product3(bank["Y"][:, 0:T], w2_hi[L][:, e, c, :], w2_lo[L][:, e, c, :],
                                 Ah[:, s, :], Al[:, s, :], e == 0 and c == 0, False)
                m.then_inc(fc2_ps[L].sem, 1)

            def fc2_bias(L, b):
                pe.wait_ge(cT_kept[L].sem, cT_kept[L].at(b, 1))
                pe.matmul(bank["Y"][:, 0:T], b2[:, L, :], combT[L][:, :], start=False, stop=True,
                          skip_group_check=True).then_inc(y_ps[L].sem, 1)

            def y_T(L, b):
                if "M" in filled:
                    sig, before, n_read = filled["M"]
                    pe.wait_ge(sig.sem, sig.at(before, n_read))
                filled["M"] = (ln[2 * L + 1], b, 1)
                pe.wait_ge(y_kept[L].sem, y_kept[L].at(b, 1))
                for blk in range(2):
                    m = pe.transpose(M[:, blk * D:(blk + 1) * D], yT[:, blk * D:(blk + 1) * D], ident[:, :])
                m.then_inc(yT_ps[L].sem, 1)

            def step(name, L, b, x):
                if name == "x_T":
                    x_T(L, b)
                if name == "qk":
                    qk(L, b)
                if name == "v":
                    v(L, b)
                if name == "scores":
                    scores(L, b, x)
                if name == "max_T":
                    max_T(L, b)
                if name == "scores_T":
                    scores_T(L, b, x)
                if name == "weigh_V":
                    weigh_V(L, b, x)
                if name == "O_T":
                    O_T(L, b, x)
                if name == "O_back":
                    O_back(L, b)
                if name == "out_proj":
                    out_proj(L, b)
                if name == "logits":
                    logits(L, b)
                if name == "weights_T":
                    weights_T(L, b)
                if name == "fc1":
                    fc1(L, b, x)
                if name == "fc2":
                    fc2(L, b, x)
                if name == "fc2_bias":
                    fc2_bias(L, b)
                if name == "y_T":
                    y_T(L, b)

            for t in range(FIRST, LOOP_FROM):
                for name, L, k, x in PLAN:
                    if active(t, k):
                        step(name, L, Batch(None, t - k), x)
            with pe.Fori(0, (LOOP_TO - LOOP_FROM) // 2) as reg:
                for k, (sig, before, n) in filled.items():
                    filled[k] = (sig, Batch(reg, before.c), n)
                for w in range(2):
                    for name, L, k, x in PLAN:
                        step(name, L, Batch(reg, LOOP_FROM + w - k), x)
            for k, (sig, before, n) in filled.items():
                filled[k] = (sig, Batch(None, before.c + LOOP_TO - LOOP_FROM - 2), n)
            for t in range(LOOP_TO, LAST + 1):
                for name, L, k, x in PLAN:
                    if active(t, k):
                        step(name, L, Batch(None, t - k), x)

        @block.vector
        def _(dve):
            dve.wait_ge(w_in.sem, SMALL_LOADS * DMA)
            dve.tensor_copy(identb[:, :], ident[:, :]).then_inc(const_dve.sem, 1)
            for i, (_, a, z, hi, lo, mult) in enumerate(weight_pieces):
                w = stage[i % 2][:, 0:z - a]
                dve.wait_ge(wst_in[i % 2].sem, (i // 2 + 1) * DMA)
                if mult:
                    units = slice(C_MULT + a // D, C_MULT + z // D)
                    w3 = w.rearrange("p (u n) -> p u n", n=D)
                    dve.tensor_tensor(w3, w3, cols[:, units].unsqueeze(2).broadcast_to((D, (z - a) // D, D)),
                                      ALU.mult).then_inc(w_scaled.sem, 1)
                    dve.wait_ge(w_scaled.sem, scaled_before[i])
                dve.wait_ge(w_hi_done.sem, i + 1)
                dve.tensor_tensor(lo, w, hi.bitcast(F32), ALU.subtract).then_inc(w_lo_done.sem, 1)
            dve.wait_ge(const_dve.sem, 1)
            dve.wait_ge(const_pool.sem, len(CONSTANTS))

            M = bank["M"]

            def x_T_split(s, b, j):
                hi, lo = xTh[split_of(s)], xTl[split_of(s)]
                if j == 0:
                    dve.wait_ge(xT_kept[s].sem, xT_kept[s].at(b, 1))
                    if s == 1:
                        if b.after(1):
                            dve.wait_ge(h_ps[0].sem, h_ps[0].at(b, E0, back=1))
                    elif s == 3:
                        if b.after(1):
                            dve.wait_ge(h_ps[1].sem, h_ps[1].at(b, U1, back=1))
                    elif s == 0:
                        prev = Batch(b.reg, b.c + K_A0PREP - 1 - K_A1PREP)
                        if prev.exists():
                            dve.wait_ge(qk_ps[1].sem, qk_ps[1].at(prev, 1))
                    else:
                        prev = Batch(b.reg, b.c + K_A1PREP - K_A0PREP)
                        if prev.exists():
                            dve.wait_ge(qk_ps[0].sem, qk_ps[0].at(prev, 1))
                    dve.tensor_copy(hi[:, :], xT[:, :]).then_inc(xT_split[s].sem, 1)
                else:
                    dve.wait_ge(xT_split[s].sem, xT_split[s].at(b, 1))
                    dve.tensor_tensor(lo[:, :], xT[:, :], hi[:, :].bitcast(F32), ALU.subtract)\
                        .then_inc(xT_split[s].sem, 1)

            def qk_part(L, b, j):
                if j == 0:
                    dve.wait_ge(qk_kept[L].sem, qk_kept[L].at(b, qk_kept[L].per))
                    other = Batch(b.reg, b.c + (K_A0PREP - 1 - K_A1PREP if L == 0 else K_A1PREP - K_A0PREP))
                    if other.exists():
                        dve.wait_ge(qk_written[1 - L].sem, qk_written[1 - L].at(other, 6 * DMA))
                    if b.after(1):
                        dve.wait_ge(qk_written[L].sem, qk_written[L].at(b, 6 * DMA, back=1))
                else:
                    dve.wait_ge(qk_parts[L].sem, qk_parts[L].at(b, j))
                if j in (0, 2):
                    ins = dve.tensor_copy(parts[:, j // 2, :], u[:, :])
                elif j == 1:
                    ins = dve.tensor_tensor(u[:, :], u[:, :], parts[:, 0, :], ALU.subtract)
                else:
                    ins = dve.tensor_tensor(parts[:, 2, :], u[:, :], parts[:, 1, :], ALU.subtract)
                ins.then_inc(qk_parts[L].sem, 1)

            def v_keep(L, b):
                dve.wait_ge(v_ps[L].sem, v_ps[L].at(b, 1))
                if b.after(1):
                    dve.wait_ge(o_ps[L].sem, o_ps[L].at(b, 4, back=1))
                for blk in range(2):
                    o = V[L][:, blk, 0:NH * VW].rearrange("p (h w) -> p h w", w=VW)[:, :, 0:HD]
                    a = M[:, blk * D:(blk + 1) * D].rearrange("p (h w) -> p h w", w=HD)
                    if L == 0:
                        ins = dve.tensor_copy(o, a)
                    else:
                        ins = dve.tensor_tensor(o, a, rows[:, R_BV:R_BV + D].rearrange("p (h w) -> p h w", w=HD), ALU.add)
                ins.then_inc(v_kept[L].sem, 1)

            def row_max(L, b, h):
                dve.wait_ge(s_ps[L].sem, s_ps[L].at(b, h + 1))
                if h == 0:
                    if b.after(1):
                        dve.wait_ge(mT_ps[L].sem, mT_ps[L].at(b, 1, back=1))
                S = bank[("S", "H0", "H1")[h % 3] if L == 0 else "S"]
                n = 2 if L == 1 else 3
                w = T if L == 1 else D
                dve.tensor_reduce(mp[L][:, :, h], S[:, 0:n * w].rearrange("p (a c) -> p a c", a=n),
                                  AX.X, ALU.max).then_inc(maxed[L].sem, 1)

            def max_join(L, b):
                if L == 0:
                    dve.wait_ge(maxed[0].sem, maxed[0].at(b, NH))
                    dve.tensor_tensor(mp[0][:, 1, :], mp[0][:, 1, :], mp[0][:, 2, :], ALU.max)\
                        .then_inc(maxed[0].sem, 1)

            def max_parts(L, b):
                dve.wait_ge(mT_ps[L].sem, mT_ps[L].at(b, 1))
                other = Batch(b.reg, b.c + (K_A0PREP - K_A1 if L == 0 else K_A1 - 1 - K_A0PREP))
                if other.exists():
                    dve.wait_ge(m_written[1 - L].sem, m_written[1 - L].at(other, DMA))
                if b.after(1):
                    dve.wait_ge(m_written[L].sem, m_written[L].at(b, DMA, back=1))
                dve.tensor_scalar(mrow[:, 0, :], M[0:NH, 0:T], -1.0, None, ALU.mult).then_inc(m_parts[L].sem, 1)
                dve.wait_ge(m_parts[L].sem, m_parts[L].at(b, 1))
                dve.scalar_tensor_tensor(out=mrow[:, 1, :], in0=M[0:NH, 0:T], scalar=-1.0, in1=mrow[:, 0, :],
                                         op0=ALU.mult, op1=ALU.subtract).then_inc(m_parts[L].sem, 1)

            def keep_O(L, b, g):
                dve.wait_ge(o_ps[L].sem, o_ps[L].at(b, g + 1))
                if g == 0:
                    other = Batch(b.reg, b.c + (K_A0 - 1 - K_A1 if L == 0 else K_A1 - K_A0))
                    if other.exists():
                        dve.wait_ge(oT_ps[1 - L].sem, oT_ps[1 - L].at(other, 2))
                    if b.after(1):
                        dve.wait_ge(oT_ps[L].sem, oT_ps[L].at(b, 2, back=1))
                dve.tensor_copy(OT[:, g, :], bank["O"][:, 0:T]).then_inc(o_kept[L].sem, 1)

            def O_inverse(L, b, blk):
                dve.wait_ge(oT_ps[L].sem, oT_ps[L].at(b, blk + 1))
                dve.reciprocal(oinv[:, blk, :], M[:, :].rearrange("p (h w) -> p h w", w=32)[:, :, HD])\
                    .then_inc(o_norm[L].sem, 1)

            def O_norm(L, b, blk):
                dve.wait_ge(o_norm[L].sem, o_norm[L].at(b, 2 * blk + 1))
                dve.tensor_tensor(On[:, blk, :].rearrange("p (h w) -> p h w", w=HD),
                                  M[:, :].rearrange("p (h w) -> p h w", w=32)[:, :, 0:HD],
                                  oinv[:, blk, :].unsqueeze(2).broadcast_to((D, NH, HD)), ALU.mult)\
                    .then_inc(o_norm[L].sem, 1)

            def add_up(site, b):
                if site % 2 == 0:
                    dve.wait_ge(proj_ps[site // 2].sem, proj_ps[site // 2].at(b, 1))
                else:
                    dve.wait_ge(yT_ps[site // 2].sem, yT_ps[site // 2].at(b, 1))
                if site == 0:
                    wait_x(dve, b)
                if site == 2:
                    dve.wait_ge(bias_added.sem, bias_added.at(b, 1))
                if site == 3:
                    if b.after(1):
                        dve.wait_ge(out_stored.sem, out_stored.at(b, DMA, back=1))
                dst = norm_out(site)[b.p]
                dve.tensor_tensor(dst[:, :, :], M[:, 0:T].rearrange("p (c d) -> p c d", c=2),
                                  stage_in(site)[b.p][:, :, :], ALU.add).then_inc(ln[site].sem, 1)

            def stats(site, b, blk):
                dve.wait_ge(ln[site].sem, ln[site].at(b, 1))
                dve.bn_stats(st6[:, site, blk, :], norm_out(site)[b.p][:, blk, :]).then_inc(ln[site].sem, 1)

            def aggregate(site, b, blk):
                dve.wait_ge(ln[site].sem, ln[site].at(b, 2 + blk))
                if blk == 0:
                    if b.after(1):
                        dve.wait_ge(ln_pool[site].sem, ln_pool[site].at(b, 2, back=1))
                take_wait(dve)
                dve.bn_aggr(mv[:, site, blk, :], st6[:, site, blk, :]).then_inc(ln[site].sem, 1)

            def normalise(site, b, blk):
                if blk == 0:
                    dve.wait_ge(ln_pool[site].sem, ln_pool[site].at(b, 2))
                z = norm_out(site)[b.p][:, blk, :]
                dve.tensor_scalar(z, z, mv[:, site, blk, 0:1], rstd[:, site, blk:blk + 1],
                                  ALU.subtract, ALU.mult).then_inc(ln[site].sem, 1)

            def top_step(L, b, j):
                n = EXPERTS[L]
                blk = j % 2
                i2 = iota[:, 0:n]
                sig = top[L]
                if j == 0:
                    dve.wait_ge(lg_ps[L].sem, lg_ps[L].at(b, 1))
                    if b.after(1):
                        dve.wait_ge(gexp[L].sem, gexp[L].at(b, 2, back=1))
                    src = M[:, 0:2 * n].rearrange("p (c e) -> p c e", c=2)
                    if L == 0:
                        dve.tensor_tensor(lg[0][:, :, :], src, rows[:, R_GB:R_GB + E0].unsqueeze(1).broadcast_to((D, 2, E0)),
                                          ALU.add).then_inc(sig.sem, 1)
                    else:
                        dve.tensor_copy(lg[1][:, :, :], src).then_inc(sig.sem, 1)
                elif j in (1, 2):
                    dve.wait_ge(sig.sem, sig.at(b, 1))
                    take_wait(dve)
                    dve.max(m8[L][:, j - 1, :], lg[L][:, j - 1, :]).then_inc(sig.sem, 1)
                elif j == 3:
                    dve.wait_ge(sig.sem, sig.at(b, 3))
                    dve.tensor_scalar(gs[L][:, 0, :], m8[L][:, :, 0], -1.0, None, ALU.mult).then_inc(sig.sem, 1)
                elif j == 4:
                    dve.wait_ge(gexp[L].sem, gexp[L].at(b, 2))
                    dve.reciprocal(gs[L][:, 2, :], gs[L][:, 1, :]).then_inc(sig.sem, 1)
                elif j in (5, 6):
                    c = j - 5
                    dve.wait_ge(sig.sem, sig.at(b, 5))
                    dve.tensor_scalar(pe_[L][:, c, :], pe_[L][:, c, :], gs[L][:, 2, c:c + 1], None, ALU.mult)\
                        .then_inc(sig.sem, 1)
                elif j in (7, 8):
                    c = j - 7
                    dve.wait_ge(sig.sem, sig.at(b, 6 + c))
                    take_wait(dve)
                    dve.max(m8[L][:, c, :], pe_[L][:, c, :]).then_inc(sig.sem, 1)
                elif j in (9, 10):
                    c = j - 9
                    dve.wait_ge(sig.sem, sig.at(b, 8 + c))
                    take_wait(dve)
                    dve.max_index(ix[L][:, c, :], m8[L][:, c, :], pe_[L][:, c, :]).then_inc(sig.sem, 1)
                elif j == 11:
                    dve.wait_ge(sig.sem, sig.at(b, 11))
                    dve.tensor_copy(ixf[L][:, :, :], ix[L][:, :, :]).then_inc(sig.sem, 1)
                elif j in (12, 13):
                    c = j - 12
                    dve.wait_ge(sig.sem, sig.at(b, 12))
                    dve.tensor_scalar(mk[L][:, c, :], i2, ixf[L][:, c, 0:1], None, ALU.is_equal)\
                        .then_inc(sig.sem, 1)
                elif j in (14, 15) or (L == 1 and j in (16, 17)):
                    kth = (j - 12) // 2
                    c = j % 2
                    dve.wait_ge(sig.sem, sig.at(b, j - 1))
                    dve.scalar_tensor_tensor(out=mk[L][:, c, :], in0=i2, scalar=ixf[L][:, c, kth:kth + 1],
                                             in1=mk[L][:, c, :], op0=ALU.is_equal, op1=ALU.add)\
                        .then_inc(sig.sem, 1)
                elif j == (16 if L == 0 else 18):
                    dve.wait_ge(sig.sem, sig.at(b, j))
                    if b.after(1):
                        dve.wait_ge(cT_ps[L].sem, cT_ps[L].at(b, 1, back=1))
                    dve.tensor_tensor(comb[L][:, :, 0:n], mk[L][:, :, :], pe_[L][:, :, :], ALU.mult)\
                        .then_inc(sig.sem, 1)
                elif j == 19:
                    dve.wait_ge(sig.sem, sig.at(b, 19))
                    dve.tensor_reduce(gs[1][:, 3, :], comb[1][:, :, 0:n], AX.X, ALU.add).then_inc(sig.sem, 1)
                elif j == 20:
                    dve.wait_ge(sig.sem, sig.at(b, 20))
                    dve.tensor_scalar(gs[1][:, 3, :], gs[1][:, 3, :], 1e-20, None, ALU.add).then_inc(sig.sem, 1)
                elif j == 21:
                    dve.wait_ge(sig.sem, sig.at(b, 21))
                    dve.reciprocal(gs[1][:, 3, :], gs[1][:, 3, :]).then_inc(sig.sem, 1)
                else:
                    c = j - 22
                    dve.wait_ge(sig.sem, sig.at(b, 22))
                    dve.tensor_scalar(comb[1][:, c, 0:n], comb[1][:, c, 0:n], gs[1][:, 3, c:c + 1], None, ALU.mult)\
                        .then_inc(sig.sem, 1)

            def times(b, e):
                dve.wait_ge(acted[1].sem, acted[1].at(b, e + 1))
                H = bank[("H0", "H1", "ST0", "ST1")[e % 4]]
                if e >= 6:
                    dve.wait_ge(lo_done[1].sem, lo_done[1].at(b, e - 5))
                dve.scalar_tensor_tensor(out=R[:, e % 6, :], in0=H[:, 0:T],
                                         scalar=cols[:, C_FC1 + 2 * e:C_FC1 + 2 * e + 1],
                                         in1=ge[:, (e % 4) * T:(e % 4 + 1) * T], op0=ALU.add, op1=ALU.mult)\
                    .then_inc(timed.sem, 1)

            def act_lo(L, b, e):
                dve.wait_ge(hi_done[L].sem, hi_done[L].at(b, e + 1))
                depth = (3, 6)[L]
                if e >= depth:
                    dve.wait_ge(fc2_ps[L].sem, fc2_ps[L].at(b, e - depth + 1))
                s = slice(2 * (e % 3), 2 * (e % 3) + 2) if L == 0 else slice(e % 6, e % 6 + 1)
                dve.tensor_tensor(Al[:, s, :], R[:, s, :], Ah[:, s, :].bitcast(F32), ALU.subtract)\
                    .then_inc(lo_done[L].sem, 1)

            def step(name, L, b, x):
                if name == "x_T_split":
                    x_T_split(L, b, x)
                if name == "qk_part":
                    qk_part(L, b, x)
                if name == "v_keep":
                    v_keep(L, b)
                if name == "row_max":
                    row_max(L, b, x)
                if name == "max_join":
                    max_join(L, b)
                if name == "max_parts":
                    max_parts(L, b)
                if name == "keep_O":
                    keep_O(L, b, x)
                if name == "O_inverse":
                    O_inverse(L, b, x)
                if name == "O_norm":
                    O_norm(L, b, x)
                if name == "sum":
                    add_up(L, b)
                if name == "stats":
                    stats(L, b, x)
                if name == "aggregate":
                    aggregate(L, b, x)
                if name == "normalise":
                    normalise(L, b, x)
                if name == "top":
                    top_step(L, b, x)
                if name == "times":
                    times(b, x)
                if name == "act_lo":
                    act_lo(L, b, x)

            run_slots(dve, step)


def kernel(**inputs):
    import numpy as np
    import concourse.bacc as bacc
    import ml_dtypes
    from concourse.bass_utils import run_bass_kernel_spmd

    a = {k: np.asarray(v) for k, v in inputs.items()}

    def flat(w):
        return np.ascontiguousarray(w.reshape(w.shape[0], -1))

    fc1 = a["L1_ffn_fc1_w"].reshape(E1, 2, D, D)
    s1 = a["L1_ffn_s_fc1_w"].reshape(2, 2, D, D).transpose(1, 0, 2, 3)
    fc1 = np.concatenate([fc1, s1], axis=0)
    fc1b = np.concatenate([a["L1_ffn_fc1_b"].reshape(E1, 2, D),
                           a["L1_ffn_s_fc1_b"].reshape(2, 2, D).transpose(1, 0, 2)], axis=0)
    mult = np.concatenate([a["L1_ffn_geglu_mult"], a["L1_ffn_s_geglu_mult"].reshape(2, D)], axis=0)
    fc2 = np.concatenate([a["L1_ffn_fc2_w"], a["L1_ffn_s_fc2_w"].reshape(D, 2, D).transpose(1, 0, 2)], axis=0)
    w_in = a["L1_attn_w_in"].transpose(1, 0)
    qkv = a["L0_attn_w_qkv"]
    b_in = a["L1_attn_b_in"]
    neg = np.float32(NEG)
    key_after = np.arange(D)[None, :] > np.arange(D)[:, None]
    mask_qk = np.where(key_after, neg, np.float32(0)).astype(ml_dtypes.bfloat16)
    arrays = {
        "x_in": a["L0_attn_x"],
        "cols_in": np.concatenate([a["L0_ffn_b1"].reshape(2 * E0, D).transpose(1, 0),
                                   fc1b.reshape(2 * U1, D).transpose(1, 0), mult.transpose(1, 0),
                                   b_in[0:2 * D].reshape(2, D).transpose(1, 0)], axis=1),
        "rows_in": np.concatenate([a["L0_ffn_gate_b"], b_in[2 * D:], a["L1_attn_b_out"]]),
        "wqk0_in": qkv[:, 0:2 * D],
        "wvo0_in": np.concatenate([qkv[:, 2 * D:], a["L0_attn_w_out"]], axis=1),
        "wqk1_in": w_in[:, 0:2 * D],
        "wvo1_in": np.concatenate([w_in[:, 2 * D:], a["L1_attn_w_out"].transpose(1, 0)], axis=1),
        "gw_in": np.concatenate([a["L0_ffn_gate_w"], a["L1_ffn_gate_w"].transpose(1, 0)], axis=1),
        "w1_0_in": flat(a["L0_ffn_w1"].transpose(1, 0, 2)),
        "w2_0_in": flat(a["L0_ffn_w2"].reshape(E0, 2, D, D).transpose(2, 0, 1, 3)),
        "w1_1_in": flat(fc1.transpose(3, 0, 1, 2)),
        "w2_1_in": flat(fc2.transpose(2, 0, 1)),
        "b2_0_in": a["L0_ffn_b2"],
        "b2_1_in": np.concatenate([a["L1_ffn_fc2_b"], a["L1_ffn_s_fc2_b"].reshape(1, D)], axis=0),
        "ident_in": np.eye(D, dtype=np.float32),
        "masks_in": np.concatenate([mask_qk, mask_qk.transpose(1, 0)], axis=1),
    }
    arrays = {k: np.ascontiguousarray(v) for k, v in arrays.items()}
    nc = bacc.Bacc("TRN2", target_bir_lowering=False, num_devices=1)
    args = {k: nc.dram_tensor(k, v.shape, mybir.dt.from_np(v.dtype), kind="ExternalInput").ap()
            for k, v in arrays.items()}
    out = nc.dram_tensor("out", (NB, T, D), F32, kind="ExternalOutput").ap()
    build(nc, **args, out=out)
    r = run_bass_kernel_spmd(nc, [arrays], core_ids=[0])
    return r.results[0]["out"]
```

```python
from contextlib import ExitStack

import concourse.bass as bass
from concourse import mybir

F32 = mybir.dt.float32
F32R = mybir.dt.float32r
BF16 = mybir.dt.bfloat16
U32 = mybir.dt.uint32
ALU = mybir.AluOpType
ACT = mybir.ActivationFunctionType
AX = mybir.AxisListType

NB = 16
T = 256
D = 128
NH = 16
HD = D // NH
SCALE = float(HD) ** -0.5
E0, E1 = 8, 15
U1 = E1 + 2
EXPERTS = (E0, E1)
UNITS = (E0, U1)
EPS = 1e-5
NEG = -1e38
VW = HD + 1
TOPK = (2, 3)
RING = (4, 5)

C_B1 = 0
C_FC1 = C_B1 + 2 * E0
C_MULT = C_FC1 + 2 * U1
C_BQK = C_MULT + U1
NCOLS = C_BQK + 2
R_GB = 0
R_BV = R_GB + E0
R_BO = R_BV + D
NROWS = R_BO + D

PIECES = (0, 1, 2)
DMA = 16

K_A0PREP, K_A0, K_F0, K_A1PREP, K_A1, K_F1, K_OUT = -1, 0, 1, 1, 2, 3, 4
FIRST, LAST = -1, NB - 1 + K_OUT
LOOP_FROM, LOOP_TO = 5, 15


def top_ops(L):
    return 11 if L == 0 else 15


def plan(slots):
    s = []
    latest = {}

    def add(at, name, L, k, x=0, chain=None):
        if chain is not None:
            at = latest[chain, L, k] = max(at, latest.get((chain, L, k), at))
        s.append((at, len(s), name, L, k, x))

    def attention(at, L, k, step, lag):
        for h in range(NH):
            add(at + h * step, "scores_T", L, k, h)
            add(at + h * step + 0.1, "exp", L, k, h)
            if h % 4 == 3:
                add(at + h * step + lag[0], "weigh_V", L, k, h // 4)
                add(at + h * step + lag[1], "keep_O", L, k, h // 4)

    def maxima(at, step, L, k, lag):
        for h in range(NH):
            add(at + h * step, "scores", L, k, h)
            add(at + h * step + 0.05, "row_max", L, k, h)
        end = at + NH * step
        add(end + lag[0], "max_join", L, k)
        add(end + lag[1], "max_T", L, k)
        add(end + lag[2], "max_parts", L, k)
        add(end + lag[3], "max_rows", L, k)

    def prepare(at, L, k, lag):
        add(at, "x_T", 2 * L, k)
        add(at + 0.05, "x_T_keep", 2 * L, k)
        add(at + lag[1], "x_T_lo", 2 * L, k)
        if L == 1:
            add(at + lag[1], "residual_bias", L, k)
        add(at + lag[2], "qk", L, k)
        add(at + lag[3], "qk_keep", L, k)
        add(at + lag[4], "v", L, k)
        for j in range(1, 4):
            add(at + lag[5] + lag[6] * j, "qk_part", L, k, j, chain="qk")
        add(at + lag[7], "v_keep", L, k)
        add(at + lag[8], "parts_store", L, k)
        add(at + lag[9], "stack", L, k)

    def norm(at, site, k, lag):
        add(at, "sum", site, k, chain="norm")
        for blk in range(2):
            add(at + lag[0] + 0.1 * blk, "stats", site, k, blk, chain="norm")
        for blk in range(2):
            add(at + lag[1] + 0.1 * blk, "aggregate", site, k, blk, chain="norm")
        add(at + lag[1] + 0.1, "inverse_std", site, k, chain="norm")
        for blk in range(2):
            add(at + lag[2] + 0.1 * blk, "normalise", site, k, blk, chain="norm")

    def after_attention(at, L, k, lag, norm_lag):
        for blk in range(2):
            add(at + lag[0] * blk, "O_T", L, k, blk)
            add(at + lag[0] * blk + lag[1], "O_inverse", L, k, blk, chain="O")
            add(at + lag[0] * blk + lag[2], "O_norm", L, k, blk, chain="O")
        add(at + lag[3], "O_back", L, k)
        add(at + lag[4], "O_back_keep", L, k)
        add(at + lag[5], "out_proj", L, k)
        norm(at + lag[6], 2 * L, k, norm_lag)

    def gate(at, L, k, lag):
        add(at, "x_T", 2 * L + 1, k)
        add(at + 0.05, "x_T_keep", 2 * L + 1, k)
        add(at + lag[1], "x_T_lo", 2 * L + 1, k)
        add(at + lag[2], "logits", L, k)
        for j in range(4):
            add(at + lag[3] + lag[4] * j, "top", L, k, j, chain="top")
        add(at + lag[5], "gate_exp", L, k)
        n = top_ops(L)
        for j in range(4, n):
            add(at + lag[6] + lag[7] * (j - 4) / (n - 4), "top", L, k, j, chain="top")
        add(at + lag[8], "weights_T", L, k)
        add(at + lag[9], "weights_T_keep", L, k)
        add(at + lag[10], "weights_store", L, k)
        for e in range(RING[L]):
            add(at + lag[11], "weights_load", L, k, e)

    def after_experts(at, L, k, lag, norm_lag):
        add(at, "y_keep", L, k)
        add(at + lag[0], "y_T", L, k)
        norm(at + lag[1], 2 * L + 1, k, norm_lag)

    def experts(at, L, k, step, lag):
        for e in range(UNITS[L]):
            add(at + e * step, "fc1", L, k, e)
            add(at + e * step + 0.1, "activate", L, k, e)
            if L == 1:
                add(at + e * step + lag[0], "times", L, k, e)
            if e < EXPERTS[L]:
                add(at + e * step + lag[1], "weigh", L, k, e)
                if e + RING[L] < EXPERTS[L]:
                    add(at + e * step + lag[1] + 0.01, "weights_load", L, k, e + RING[L])
            add(at + e * step + lag[2], "act_hi", L, k, e)
            add(at + e * step + lag[3], "act_lo", L, k, e)
            add(at + e * step + lag[4], "fc2", L, k, e)
        add(at + (UNITS[L] - 1) * step + lag[4] + 0.01, "fc2_bias", L, k)

    if slots == "full":
        P2, P3 = 19.58, 42.39
        after_experts(0.45, 1, K_OUT, (0.25, 1.56), (0.00, 0.00, 3.21))
        add(1.34, "store_out", 1, K_OUT)
        add(1.75, "load_x", 0, K_A0PREP)
        attention(0.01, 0, K_A0, 1.01, (3.93, 4.90))
        experts(0.66, 0, K_F0, 2.20, (0, 0.06, 1.83, 2.50, 4.99))
        maxima(0.28, 0.98, 1, K_A1, (0.16, 0.00, 0.00, 0.09))
        gate(2.99, 1, K_F1, (0.39, 1.36, 1.47, 1.63, 0.01, 3.78, 2.86, 3.91, 7.41, 7.09, 7.55, 11.85))
        prepare(11.49, 0, K_A0PREP, (0.00, 0.00, 1.23, 0.88, 6.62, 1.54, 0.00, 7.24, 4.36, 5.74))
        attention(P2, 1, K_A1, 0.98, (2.00, 2.50))
        after_experts(P2 + 2.92, 0, K_F0, (0.61, 0.58), (0.49, 0.63, 1.41))
        after_attention(P2 + 2.93, 0, K_A0, (0.41, 0.00, 0.20, 1.62, 0.81, 2.62, 2.51), (0.04, 0.82, 2.01))
        gate(P2 + 10.25, 0, K_A0, (0.85, 0.02, 1.09, 0.18, 0.30, 2.60, 0.96, 3.10, 5.54, 5.88, 1.51, 11.42))
        maxima(P2 + 4.29, 0.77, 0, K_A0PREP, (0.41, 1.00, 1.06, 1.70))
        experts(P3, 1, K_F1, 0.65, (0.63, 0.72, 2.52, 3.44, 6.78))
        prepare(P3 + 1.45, 1, K_A1PREP, (1.66, 0.70, 2.11, 2.32, 3.10, 2.39, 0.35, 2.96, 3.52, 14.25))
        after_attention(P3 + 5.90, 1, K_A1, (0.71, 1.10, 1.65, 4.74, 3.79, 5.26, 6.80), (1.38, 4.12, 4.74))
    elif slots == "first":
        P2, P3 = 18.75, 39.70
        add(2.38, "load_x", 0, K_A0PREP)
        attention(0.00, 0, K_A0, 1.01, (2.44, 2.24))
        experts(0.45, 0, K_F0, 1.97, (0, 0.59, 2.64, 3.44, 6.22))
        maxima(0.33, 0.97, 1, K_A1, (1.46, 0.03, 0.00, 0.53))
        gate(3.00, 1, K_F1, (0.53, 0.65, 1.46, 1.63, 0.36, 4.65, 3.97, 3.41, 7.93, 7.72, 8.03, 8.42))
        prepare(10.98, 0, K_A0PREP, (0.09, 0.43, 1.06, 1.13, 8.07, 1.43, 0.00, 7.20, 4.61, 7.97))
        attention(P2, 1, K_A1, 0.98, (2.01, 2.87))
        after_experts(P2 + 2.70, 0, K_F0, (0.84, 0.63), (0.19, 0.31, 1.59))
        after_attention(P2 + 2.83, 0, K_A0, (0.47, 0.00, 0.18, 1.77, 2.06, 3.59, 3.61), (0.02, 0.22, 1.88))
        gate(P2 + 10.33, 0, K_A0, (0.00, 0.25, 1.33, 0.37, 0.57, 1.86, 1.02, 2.98, 5.95, 7.19, 4.83, 8.41))
        maxima(P2 + 4.24, 0.77, 0, K_A0PREP, (0.38, 1.49, 0.47, 1.39))
        experts(P3, 1, K_F1, 0.65, (0.77, 0.71, 2.28, 2.75, 7.00))
        prepare(P3 + 1.45, 1, K_A1PREP, (0.00, 0.56, 2.21, 2.18, 2.54, 2.45, 0.71, 3.71, 3.18, 14.20))
        after_attention(P3 + 6.43, 1, K_A1, (1.19, 0.40, 1.82, 4.13, 2.88, 5.25, 4.07), (0.69, 2.01, 4.21))
    else:
        P2, P3 = 14.45, 33.20
        after_experts(0.24, 1, K_OUT, (0.58, 2.26), (0.00, 0.03, 2.34))
        add(0.28, "store_out", 1, K_OUT)
        experts(0.41, 0, K_F0, 1.42, (0, 0.86, 2.77, 3.21, 4.59))
        maxima(0.39, 0.55, 1, K_A1, (1.80, 0.92, 0.00, 0.60))
        gate(5.82, 1, K_F1, (1.00, 0.69, 1.46, 1.63, 0.24, 3.85, 2.53, 3.12, 6.67, 7.36, 6.73, 8.42))
        attention(P2, 1, K_A1, 0.98, (2.01, 2.94))
        after_experts(P2 + 2.74, 0, K_F0, (1.94, 1.04), (0.39, 0.00, 1.01))
        experts(P3, 1, K_F1, 0.65, (0.60, 0.00, 2.28, 2.98, 5.73))
        prepare(P3 + 1.43, 1, K_A1PREP, (0.00, 1.12, 1.97, 1.96, 2.29, 2.29, 0.53, 2.91, 3.08, 11.97))
        after_attention(P3 + 6.46, 1, K_A1, (0.68, 0.00, 1.21, 2.83, 2.77, 4.36, 4.38), (0.72, 3.21, 4.32))
    s.sort()
    return [x[2:] for x in s]


PLANS = {slots: plan(slots) for slots in ("first", "full", "last")}


def plan_of(t):
    return PLANS["first" if t < K_OUT else "last" if t >= NB else "full"]


BANKS = ("ST0", "ST1", "S", "O", "M", "H0", "H1", "Y")


def active(t, k):
    return 0 <= t - k < NB


class Batch:

    def __init__(self, reg, c):
        self.reg, self.c, self.p = reg, c, c % 2

    def after(self, back):
        return self.reg is not None or self.c >= back

    def exists(self):
        return self.reg is not None or 0 <= self.c < NB

    def row(self):
        return self.c if self.reg is None else self.reg * 2 + self.c


class Signal:

    def __init__(self, sem, per):
        self.sem, self.per = sem, per

    def at(self, b, n, back=0):
        if b.reg is None:
            return (b.c - back) * self.per + n
        return b.reg * (2 * self.per) + ((b.c - back) * self.per + n)


def run_slots(eng, step):
    for t in range(FIRST, LOOP_FROM):
        for name, L, k, x in plan_of(t):
            if active(t, k):
                step(name, L, Batch(None, t - k), x)
    with eng.Fori(0, (LOOP_TO - LOOP_FROM) // 2) as reg:
        for u in range(2):
            for name, L, k, x in PLANS["full"]:
                step(name, L, Batch(reg, LOOP_FROM + u - k), x)
    for t in range(LOOP_TO, LAST + 1):
        for name, L, k, x in plan_of(t):
            if active(t, k):
                step(name, L, Batch(None, t - k), x)


def build(nc, x_in, cols_in, rows_in, wqk0_in, wvo0_in, wqk1_in, wvo1_in, gw_in,
          w1_0_in, w2_0_in, w1_1_in, w2_1_in, b2_0_in, b2_1_in, ident_in, masks_in, out):
    ctx = ExitStack()
    with ctx:
        def sb(name, shape, dt=F32):
            return ctx.enter_context(nc.sbuf_tensor(name, shape, dt))

        def dram(name, shape, dt):
            return nc.dram_tensor(name, shape, dt, kind="Internal").ap()

        def signal(name, per=1):
            return Signal(ctx.enter_context(nc.semaphore(name)), per)

        def pair(name, per=1):
            return [signal(f"{name}{L}", per) for L in range(2)]

        wqk_hi = sb("wqk_hi", [D, 2, 2 * D], F32R)
        wqk_lo = sb("wqk_lo", [D, 2, 2 * D], F32R)
        wvo = sb("wvo", [D, 2, 2, D])
        gw = sb("gw", [D, E0 + E1])
        w1_hi = [sb("w1_hi0", [D, E0, 2, D], F32R), sb("w1_hi1", [D, U1, 2, D], F32R)]
        w1_lo = [sb("w1_lo0", [D, E0, 2, D], F32R), sb("w1_lo1", [D, U1, 2, D], F32R)]
        w2_hi = [sb("w2_hi0", [D, E0, 2, D], F32R), sb("w2_hi1", [D, U1, 1, D], F32R)]
        w2_lo = [sb("w2_lo0", [D, E0, 2, D], F32R), sb("w2_lo1", [D, U1, 1, D], F32R)]
        b2 = sb("b2", [D, 2, D])
        cols = sb("cols", [D, NCOLS])
        rows = sb("rows", [D, NROWS])
        ident = sb("ident", [D, D])
        identb = sb("identb", [D, D], BF16)
        masks = sb("masks", [D, 2, D], BF16)
        iota = sb("iota", [D, E1])
        minus_half = sb("minus_half", [D, 2])
        eps = sb("eps", [D, 2])
        Qs = [sb(f"Qs{L}", [D, NH, T], BF16) for L in range(2)]
        Ks = [sb(f"Ks{L}", [D, NH, T], BF16) for L in range(2)]
        V = [sb(f"V{L}", [D, 2, NH * VW + 32 - VW]) for L in range(2)]
        P = sb("P", [D, 2, 4, 2 * T])
        OT = sb("OT", [D, 4, T])
        On = sb("On", [D, 2, D])
        OnT = sb("OnT", [D, T])
        xT = sb("xT", [D, T])
        xTh = [sb(f"xTh{s}", [D, T], F32R) for s in range(3)]
        xTl = [sb(f"xTl{s}", [D, T], F32R) for s in range(3)]
        u = sb("u", [D, 2 * T])
        parts = sb("parts", [D, 3, 2 * T], BF16)
        mp = [sb("mp0", [D, 3, NH]), sb("mp1", [D, 2, NH])]
        mrow = sb("mrow", [NH, 2, T], BF16)
        oinv = sb("oinv", [D, 2, NH])
        xa = [[sb(f"xa{L}{p}", [D, 2, D]) for p in range(2)] for L in range(2)]
        xb = [[sb(f"xb{L}{p}", [D, 2, D]) for p in range(2)] for L in range(2)]
        xo = sb("xo", [D, 2, D])
        st6 = sb("st6", [D, 4, 2, 6])
        mv = sb("mv", [D, 4, 2, 2])
        rstd = sb("rstd", [D, 4, 2])
        lg = [sb(f"lg{L}", [D, 2, EXPERTS[L]]) for L in range(2)]
        pe_ = [sb(f"pe{L}", [D, 2, EXPERTS[L]]) for L in range(2)]
        eq = [sb(f"eq{L}", [D, 2, TOPK[L], EXPERTS[L]]) for L in range(2)]
        mk = [sb(f"mk{L}", [D, 2, EXPERTS[L]]) for L in range(2)]
        m8 = [sb(f"m8{L}", [D, 2, 8]) for L in range(2)]
        ix = [sb(f"ix{L}", [D, 2, 8], U32) for L in range(2)]
        gs = [sb(f"gs{L}", [D, 4, 2]) for L in range(2)]
        comb = [sb(f"comb{L}", [D, 2, D]) for L in range(2)]
        combT = [sb(f"combT{L}", [D, T]) for L in range(2)]
        cw = [sb(f"cw{L}", [D, RING[L], T]) for L in range(2)]
        R = sb("R", [D, 6, T])
        Ah = sb("Ah", [D, 6, T], F32R)
        Al = sb("Al", [D, 6, T], F32R)
        yT = sb("yT", [D, T])
        ge = P[:, 0, :, :].rearrange("p a b -> p (a b)")

        qk_d = [dram(f"qk_d{L}", (2, 3, HD, NH, T), BF16) for L in range(2)]
        cw_d = [dram(f"cw_d{L}", (EXPERTS[L], T), F32) for L in range(2)]

        bank = {n: ctx.enter_context(nc.psum_tensor(f"bank_{n}", [D, 512], F32)) for n in BANKS}

        w_in = signal("w_in")
        wst_in = [signal(f"wst_in{i}") for i in range(7)]
        w_scaled = signal("w_scaled")
        w_hi_done = signal("w_hi_done")
        w_lo_done = signal("w_lo_done")
        const_dve = signal("const_dve")
        const_pool = signal("const_pool")
        wait_taken = [signal("wait_taken_sp"), signal("wait_taken_dve")]
        dve_engine = nc.vector
        x_loaded = [signal(f"x_loaded{p}", DMA) for p in range(2)]
        out_stored = signal("out_stored", DMA)
        xT_ps = [signal(f"xT_ps{s}") for s in range(4)]
        xT_kept = [signal(f"xT_kept{s}") for s in range(4)]
        xT_split = [signal(f"xT_split{s}", 2) for s in range(4)]
        bias_added = signal("bias_added")
        qk_ps = pair("qk_ps")
        qk_kept = [signal("qk_kept0", 1), signal("qk_kept1", 2)]
        qk_parts = pair("qk_parts", 4)
        qk_written = pair("qk_written", 6 * DMA)
        stacked = pair("stacked", 6 * DMA)
        v_ps = pair("v_ps")
        v_kept = pair("v_kept")
        s_ps = pair("s_ps", NH)
        maxed = [signal("maxed0", NH + 1), signal("maxed1", NH)]
        mT_ps = pair("mT_ps")
        m_parts = pair("m_parts", 2)
        m_stacked = pair("m_stacked", 2 * DMA)
        st_ps = pair("st_ps", NH)
        exped = pair("exped", NH)
        o_ps = pair("o_ps", 4)
        o_kept = pair("o_kept", 4)
        oT_ps = pair("oT_ps", 2)
        o_norm = pair("o_norm", 4)
        onT_ps = pair("onT_ps")
        onT_kept = pair("onT_kept")
        proj_ps = pair("proj_ps")
        ln = [signal(f"ln{s}", 7) for s in range(4)]
        ln_pool = [signal(f"ln_pool{s}", 2) for s in range(4)]
        lg_ps = pair("lg_ps")
        top = [signal(f"top{L}", top_ops(L)) for L in range(2)]
        gexp = pair("gexp", 2)
        cT_ps = pair("cT_ps")
        cT_kept = pair("cT_kept")
        cw_stored = pair("cw_stored", DMA)
        cw_loaded = [[signal(f"cw_loaded{L}{i}", EXPERTS[L] // RING[L] * DMA) for i in range(RING[L])]
                     for L in range(2)]
        h_ps = [signal(f"h_ps{L}", UNITS[L]) for L in range(2)]
        acted = [signal("acted0", 2 * E0), signal("acted1", U1)]
        timed = signal("timed", U1)
        weighed = [signal(f"weighed{L}", EXPERTS[L]) for L in range(2)]
        hi_done = [signal(f"hi_done{L}", UNITS[L]) for L in range(2)]
        lo_done = [signal(f"lo_done{L}", UNITS[L]) for L in range(2)]
        fc2_ps = [signal(f"fc2_ps{L}", UNITS[L]) for L in range(2)]
        y_ps = pair("y_ps")
        y_kept = pair("y_kept")
        yT_ps = pair("yT_ps")

        def take_wait(eng):
            eng.sem_inc(wait_taken[int(eng is dve_engine)].sem, 1)

        def stage_in(s):
            return (xa[0], xb[0], xa[1], xb[1])[s]

        def norm_out(site):
            return (xb[0], xa[1], xb[1], (xo, xo))[site]

        def wait_stage_in(eng, s, b):
            if s == 0:
                wait_x(eng, b)
            else:
                eng.wait_ge(ln[s - 1].sem, ln[s - 1].at(b, 7))

        def wait_x(eng, b):
            if b.reg is None:
                eng.wait_ge(x_loaded[b.p].sem, (b.c // 2 + 1) * DMA)
            else:
                eng.wait_ge(x_loaded[b.p].sem, b.reg * DMA + (b.c // 2 + 1) * DMA)

        def split_of(s):
            return 0 if s % 2 == 0 else (1 if s == 1 else 2)

        STAGES = 7
        PIECE = 4 * T
        EARLY_PIECES = 10
        flat = lambda w: w[:, :, :, :].rearrange("p a b c -> p (a b c)")
        weight_pieces = []
        for L, src in ((0, wqk0_in), (1, wqk1_in)):
            weight_pieces.append((src, 0, 2 * D, wqk_hi[:, L, :], wqk_lo[:, L, :], False))
        for src, hi, lo, mult in ((w1_0_in, w1_hi[0], w1_lo[0], False), (w2_0_in, w2_hi[0], w2_lo[0], False),
                                  (w1_1_in, w1_hi[1], w1_lo[1], False), (w2_1_in, w2_hi[1], w2_lo[1], True)):
            n = src.shape[1]
            for a in range(0, n, PIECE):
                z = min(n, a + PIECE)
                weight_pieces.append((src, a, z, flat(hi)[:, a:z], flat(lo)[:, a:z], mult))
        room = [P[:, i, 2 * c:2 * c + 2, :] for i in range(2) for c in range(2)]
        room += [R[:, 0:4, :], cw[0][:, 0:4, :], cw[1][:, 0:4, :]]
        stage = [r_.rearrange("p a b -> p (a b)") for r_ in room]
        scaled_before = [sum(m for *_, m in weight_pieces[:i + 1]) for i in range(len(weight_pieces))]
        NPIECES = len(weight_pieces)
        SMALL_LOADS = 9

        def ones_of_V(L, blk):
            return V[L][:, blk, 0:NH * VW].rearrange("p (h w) -> p h w", w=VW)[:, :, HD:VW]

        CONSTANTS = [(b2[:, :, :], 0.0), (minus_half[:, :], -0.5), (eps[:, :], EPS)]
        const_of_layer = []
        for L in range(2):
            CONSTANTS += [(V[L][:, :, :], 0.0)]
            CONSTANTS += [(ones_of_V(L, blk), 1.0) for blk in range(2)]
            CONSTANTS += [(Qs[L][:, :, :], 0.0), (Ks[L][0:96, :, :], 0.0), (Ks[L][96:128, :, :], 1.0)]
            const_of_layer.append(len(CONSTANTS))
        CONSTANTS += [(comb[L][:, :, :], 0.0) for L in range(2)]
        CONSTANTS += [(comb[1][:, :, E1:E1 + 1], 1.0)]
        CONSTANTS += [(iota[:, e:e + 1], float(e)) for e in range(E1)]

        def is_first(b):
            return b.reg is None and b.c == 0

        block = ctx.enter_context(nc.Block())

        @block.sync
        def _(sp):
            for dst, src in ((cols[:, :], cols_in), (rows[:, :], rows_in.partition_broadcast(D)),
                             (ident[:, :], ident_in), (masks[:, :, :].rearrange("p a b -> p (a b)"), masks_in),
                             (gw[:, :], gw_in),
                             (wvo[:, 0, :, :].rearrange("p a b -> p (a b)"), wvo0_in),
                             (wvo[:, 1, :, :].rearrange("p a b -> p (a b)"), wvo1_in)):
                sp.dma_start(dst, src).then_inc(w_in.sem, DMA)
            sp.wait_ge(const_pool.sem, 1)
            sp.dma_start(b2[0:E0, 0, :], b2_0_in).then_inc(w_in.sem, DMA)
            sp.dma_start(b2[0:E1 + 1, 1, :], b2_1_in).then_inc(w_in.sem, DMA)
            src, a, z, _, _, _ = weight_pieces[0]
            sp.dma_start(stage[0][:, 0:z - a], src[:, a:z]).then_inc(wst_in[0].sem, DMA)

            def load_x(b):
                if b.after(2):
                    sp.wait_ge(xT_ps[0].sem, xT_ps[0].at(b, 1, back=2))
                take_wait(sp)
                if b.after(2):
                    sp.wait_ge(ln[0].sem, ln[0].at(b, 1, back=2))
                take_wait(sp)
                r = b.row()
                src = x_in[r:r + 1] if b.reg is None else x_in[bass.ds(r, 1)]
                sp.dma_start(xa[0][b.p][:, :, :],
                             src.rearrange("o (c p) d -> p (o c) d", p=D)).then_inc(x_loaded[b.p].sem, DMA)

            def parts_store(L, b):
                sp.wait_ge(qk_parts[L].sem, qk_parts[L].at(b, 4))
                take_wait(sp)
                if b.after(1):
                    sp.wait_ge(stacked[L].sem, stacked[L].at(b, 6 * DMA, back=1))
                take_wait(sp)
                for i in PIECES:
                    for side in range(2):
                        sp.dma_start(qk_d[L][side, i].rearrange("d h t -> h d t"),
                                     parts[:, i, side * T:(side + 1) * T]).then_inc(qk_written[L].sem, DMA)

            def stack(L, b):
                sp.wait_ge(qk_written[L].sem, qk_written[L].at(b, 6 * DMA))
                take_wait(sp)
                if is_first(b):
                    sp.wait_ge(const_pool.sem, const_of_layer[L])
                if b.after(1):
                    sp.wait_ge(st_ps[L].sem, st_ps[L].at(b, NH, back=1))
                take_wait(sp)
                for i in PIECES:
                    rows_ = slice(24 * i, 24 * i + 24)
                    q_src = qk_d[L][0, i].rearrange("d h t -> d (h t)").unsqueeze(0).broadcast_to((3, HD, NH * T))
                    k_src = qk_d[L][1].rearrange("i d h t -> (i d) (h t)")
                    sp.dma_start(Qs[L][rows_, :, :].rearrange("p h t -> p (h t)"), q_src)\
                        .then_inc(stacked[L].sem, DMA)
                    sp.dma_start(Ks[L][rows_, :, :].rearrange("p h t -> p (h t)"), k_src)\
                        .then_inc(stacked[L].sem, DMA)

            def max_rows(L, b):
                sp.wait_ge(m_parts[L].sem, m_parts[L].at(b, 2))
                for i in range(2):
                    sp.dma_start(Qs[L][96 + i:97 + i, :, :], mrow[:, i, :]).then_inc(m_stacked[L].sem, DMA)

            def weights_store(L, b):
                sp.wait_ge(cT_kept[L].sem, cT_kept[L].at(b, 1))
                take_wait(sp)
                for i in range(RING[L]):
                    if b.after(1):
                        sp.wait_ge(cw_loaded[L][i].sem, cw_loaded[L][i].at(b, cw_loaded[L][i].per, back=1))
                sp.dma_start(cw_d[L], combT[L][0:EXPERTS[L], :]).then_inc(cw_stored[L].sem, DMA)

            def weights_load(L, b, e):
                if e == 0:
                    sp.wait_ge(cw_stored[L].sem, cw_stored[L].at(b, DMA))
                    take_wait(sp)
                if e < RING[L]:
                    if b.after(1):
                        sp.wait_ge(weighed[L].sem, weighed[L].at(b, EXPERTS[L] - RING[L] + e + 1, back=1))
                else:
                    sp.wait_ge(weighed[L].sem, weighed[L].at(b, e - RING[L] + 1))
                sp.dma_start(cw[L][:, e % RING[L], :], cw_d[L][e].partition_broadcast(D))\
                    .then_inc(cw_loaded[L][e % RING[L]].sem, DMA)

            def store_out(b):
                sp.wait_ge(ln[3].sem, ln[3].at(b, 7))
                take_wait(sp)
                r = b.row()
                dst = out[r:r + 1] if b.reg is None else out[bass.ds(r, 1)]
                sp.dma_start(dst.rearrange("o (c p) d -> p (o c) d", p=D), xo[:, :, :])\
                    .then_inc(out_stored.sem, DMA)

            def step(name, L, b, x):
                if name == "load_x":
                    load_x(b)
                if name == "parts_store":
                    parts_store(L, b)
                if name == "stack":
                    stack(L, b)
                if name == "max_rows":
                    max_rows(L, b)
                if name == "weights_store":
                    weights_store(L, b)
                if name == "weights_load":
                    weights_load(L, b, x)
                if name == "store_out":
                    store_out(b)

            run_slots(sp, step)
            sp.wait_ge(out_stored.sem, NB * DMA)

        @block.gpsimd
        def _(pool):
            for n, (tile, value) in enumerate(CONSTANTS):
                if n:
                    pool.wait_ge(const_pool.sem, n)
                pool.memset(tile, value).then_inc(const_pool.sem, 1)
            pool.wait_ge(const_pool.sem, len(CONSTANTS))

            def inverse_std(site, b):
                pool.wait_ge(ln[site].sem, ln[site].at(b, 5))
                if b.after(1):
                    pool.wait_ge(ln[site].sem, ln[site].at(b, 7, back=1))
                pool.tensor_tensor(rstd[:, site, :], mv[:, site, :, 1], eps[:, :], ALU.add)\
                    .then_inc(ln_pool[site].sem, 1)
                pool.wait_ge(ln_pool[site].sem, ln_pool[site].at(b, 1))
                pool.tensor_tensor(rstd[:, site, :], rstd[:, site, :], minus_half[:, :], ALU.pow)\
                    .then_inc(ln_pool[site].sem, 1)

            def residual_bias(b):
                pool.wait_ge(xT_ps[2].sem, xT_ps[2].at(b, 1))
                pool.wait_ge(w_in.sem, SMALL_LOADS * DMA)
                pool.tensor_tensor(xa[1][b.p][:, :, :], xa[1][b.p][:, :, :],
                                   rows[:, R_BO:R_BO + D].unsqueeze(1).broadcast_to((D, 2, D)), ALU.add)\
                    .then_inc(bias_added.sem, 1)

            def weigh(L, b, e):
                w = cw[L][:, e % RING[L], :]
                turn = (e // RING[L] + 1) * DMA
                pool.wait_ge(cw_loaded[L][e % RING[L]].sem, cw_loaded[L][e % RING[L]].at(b, turn))
                if L == 0:
                    pool.wait_ge(acted[0].sem, acted[0].at(b, 2 * e + 2))
                    a = R[:, 2 * (e % 3):2 * (e % 3) + 2, :]
                    w = w.unsqueeze(1).broadcast_to((D, 2, T))
                else:
                    pool.wait_ge(timed.sem, timed.at(b, e + 1))
                    a = R[:, e % 6, :]
                pool.tensor_tensor(a, a, w, ALU.mult).then_inc(weighed[L].sem, 1)

            def step(name, L, b, x):
                if name == "inverse_std":
                    inverse_std(L, b)
                if name == "residual_bias":
                    residual_bias(b)
                if name == "weigh":
                    weigh(L, b, x)

            run_slots(pool, step)

        @block.scalar
        def _(act):
            def weights_hi(first, last):
                for i in range(first, last):
                    _, a, z, hi, _, mult = weight_pieces[i]
                    act.wait_ge(wst_in[i % STAGES].sem, (i // STAGES + 1) * DMA)
                    if mult:
                        act.wait_ge(w_scaled.sem, scaled_before[i])
                    act.activation(hi, stage[i % STAGES][:, 0:z - a], ACT.Copy).then_inc(w_hi_done.sem, 1)
                    n = i - 1 + STAGES
                    if i >= 1 and n < NPIECES:
                        src, a, z, _, _, _ = weight_pieces[n]
                        act.wait_ge(w_lo_done.sem, i)
                        act.dma_start(stage[n % STAGES][:, 0:z - a], src[:, a:z])\
                            .then_inc(wst_in[n % STAGES].sem, DMA)

            act.wait_ge(w_in.sem, SMALL_LOADS * DMA)
            weights_hi(0, 1)
            for i in range(1, STAGES):
                src, a, z, _, _, _ = weight_pieces[i]
                act.dma_start(stage[i][:, 0:z - a], src[:, a:z]).then_inc(wst_in[i].sem, DMA)

            def x_T_keep(s, b):
                act.wait_ge(xT_ps[s].sem, xT_ps[s].at(b, 1))
                before = Batch(b.reg, b.c + (K_A0PREP - K_F1, K_A0 - K_A0PREP, K_A1PREP - K_A0,
                                             K_F1 - 1 - K_A1PREP)[s])
                if before.exists():
                    user = (lg_ps[1], v_ps[0], lg_ps[0], v_ps[1])[s]
                    act.wait_ge(user.sem, user.at(before, 1))
                act.activation(xT[:, :], bank["M"][:, 0:T], ACT.Copy).then_inc(xT_kept[s].sem, 1)
                if s == 1:
                    if b.after(1):
                        act.wait_ge(h_ps[0].sem, h_ps[0].at(b, E0, back=1))
                elif s == 3:
                    if b.after(1):
                        act.wait_ge(h_ps[1].sem, h_ps[1].at(b, U1, back=1))
                elif s == 0:
                    prev = Batch(b.reg, b.c + K_A0PREP - 1 - K_A1PREP)
                    if prev.exists():
                        act.wait_ge(qk_ps[1].sem, qk_ps[1].at(prev, 1))
                else:
                    prev = Batch(b.reg, b.c + K_A1PREP - K_A0PREP)
                    if prev.exists():
                        act.wait_ge(qk_ps[0].sem, qk_ps[0].at(prev, 1))
                act.activation(xTh[split_of(s)][:, :], bank["M"][:, 0:T], ACT.Copy).then_inc(xT_split[s].sem, 1)

            def qk_keep(L, b):
                act.wait_ge(qk_ps[L].sem, qk_ps[L].at(b, 1))
                if L == 0:
                    act.activation(u[:, :], bank["M"][:, :], ACT.Copy).then_inc(qk_kept[0].sem, 1)
                    act.wait_ge(qk_kept[0].sem, qk_kept[0].at(b, 1))
                else:
                    for side in range(2):
                        act.activation(u[:, side * T:(side + 1) * T], bank["M"][:, side * T:(side + 1) * T],
                                       ACT.Identity, bias=cols[:, C_BQK + side:C_BQK + side + 1])\
                            .then_inc(qk_kept[1].sem, 1)
                act.wait_ge(qk_kept[L].sem, qk_kept[L].at(b, qk_kept[L].per))
                other = Batch(b.reg, b.c + (K_A0PREP - 1 - K_A1PREP if L == 0 else K_A1PREP - K_A0PREP))
                if other.exists():
                    act.wait_ge(qk_written[1 - L].sem, qk_written[1 - L].at(other, 6 * DMA))
                if b.after(1):
                    act.wait_ge(qk_written[L].sem, qk_written[L].at(b, 6 * DMA, back=1))
                act.activation(parts[:, 0, :], u[:, :], ACT.Copy).then_inc(qk_parts[L].sem, 1)

            def exp(L, b, h):
                act.wait_ge(st_ps[L].sem, st_ps[L].at(b, h + 1))
                if is_first(b) and L == 0 and h == 0:
                    act.wait_ge(w_lo_done.sem, NPIECES)
                n = 2 * T if L == 1 else 3 * D
                act.activation(P[:, (h // 4) % 2, h % 4, 0:n], bank[("ST0", "ST1")[h % 2]][:, 0:n], ACT.Exp,
                               scale=SCALE).then_inc(exped[L].sem, 1)

            def keep_O(L, b, g):
                act.wait_ge(o_ps[L].sem, o_ps[L].at(b, g + 1))
                if g == 0:
                    other = Batch(b.reg, b.c + (K_A0 - 1 - K_A1 if L == 0 else K_A1 - K_A0))
                    if other.exists():
                        act.wait_ge(oT_ps[1 - L].sem, oT_ps[1 - L].at(other, 2))
                    if b.after(1):
                        act.wait_ge(oT_ps[L].sem, oT_ps[L].at(b, 2, back=1))
                act.activation(OT[:, g, :], bank["O"][:, 0:T], ACT.Copy).then_inc(o_kept[L].sem, 1)

            def O_back_keep(L, b):
                act.wait_ge(onT_ps[L].sem, onT_ps[L].at(b, 1))
                act.activation(OnT[:, :], bank["M"][:, 0:T], ACT.Copy).then_inc(onT_kept[L].sem, 1)

            def gate_exp(L, b):
                act.wait_ge(top[L].sem, top[L].at(b, 4))
                if b.after(1):
                    act.wait_ge(top[L].sem, top[L].at(b, top_ops(L), back=1))
                for blk in range(2):
                    act.activation(pe_[L][:, blk, :], lg[L][:, blk, :], ACT.Exp, bias=gs[L][:, 0, blk:blk + 1],
                                   accum_out=gs[L][:, 1, blk:blk + 1]).then_inc(gexp[L].sem, 1)

            def weights_T_keep(L, b):
                act.wait_ge(cT_ps[L].sem, cT_ps[L].at(b, 1))
                if b.after(1):
                    act.wait_ge(y_ps[L].sem, y_ps[L].at(b, 1, back=1))
                if b.after(1):
                    act.wait_ge(cw_stored[L].sem, cw_stored[L].at(b, DMA, back=1))
                act.activation(combT[L][:, :], bank["M"][:, 0:T], ACT.Copy).then_inc(cT_kept[L].sem, 1)

            def activate(L, b, e):
                act.wait_ge(h_ps[L].sem, h_ps[L].at(b, e + 1))
                if L == 0:
                    if e >= 3:
                        act.wait_ge(lo_done[0].sem, lo_done[0].at(b, e - 2))
                    H = bank["H0"]
                    for c in range(2):
                        act.activation(R[:, 2 * (e % 3) + c, :], H[:, c * T:(c + 1) * T], ACT.Relu,
                                       bias=cols[:, C_B1 + 2 * e + c:C_B1 + 2 * e + c + 1])\
                            .then_inc(acted[0].sem, 1)
                else:
                    if e >= 4:
                        act.wait_ge(timed.sem, timed.at(b, e - 3))
                    H = bank[("H0", "H1", "ST0", "ST1")[e % 4]]
                    act.activation(ge[:, (e % 4) * T:(e % 4 + 1) * T], H[:, T:2 * T], ACT.Gelu,
                                   bias=cols[:, C_FC1 + 2 * e + 1:C_FC1 + 2 * e + 2]).then_inc(acted[1].sem, 1)

            def act_hi(L, b, e):
                if e < EXPERTS[L]:
                    act.wait_ge(weighed[L].sem, weighed[L].at(b, e + 1))
                else:
                    act.wait_ge(timed.sem, timed.at(b, e + 1))
                depth = (3, 6)[L]
                if e >= depth:
                    act.wait_ge(fc2_ps[L].sem, fc2_ps[L].at(b, e - depth + 1))
                s = slice(2 * (e % 3), 2 * (e % 3) + 2) if L == 0 else slice(e % 6, e % 6 + 1)
                act.activation(Ah[:, s, :], R[:, s, :], ACT.Copy).then_inc(hi_done[L].sem, 1)

            def y_keep(L, b):
                act.wait_ge(y_ps[L].sem, y_ps[L].at(b, 1))
                act.activation(yT[:, :], bank["Y"][:, 0:T], ACT.Copy).then_inc(y_kept[L].sem, 1)

            def step(name, L, b, x):
                if name == "x_T_keep":
                    x_T_keep(L, b)
                if name == "qk_keep":
                    qk_keep(L, b)
                    if L == 0 and is_first(b):
                        weights_hi(1, NPIECES)
                if name == "exp":
                    exp(L, b, x)
                if name == "keep_O":
                    keep_O(L, b, x)
                if name == "O_back_keep":
                    O_back_keep(L, b)
                if name == "gate_exp":
                    gate_exp(L, b)
                if name == "weights_T_keep":
                    weights_T_keep(L, b)
                if name == "activate":
                    activate(L, b, x)
                if name == "act_hi":
                    act_hi(L, b, x)
                if name == "y_keep":
                    y_keep(L, b)

            run_slots(act, step)

        @block.tensor
        def _(pe):
            pe.wait_ge(w_in.sem, SMALL_LOADS * DMA)
            pe.wait_ge(const_dve.sem, 1)
            pe.wait_ge(w_lo_done.sem, 1)

            def product3(o, w_hi, w_lo, a_hi, a_lo, start, stop):
                nc.tensor.matmul(o, w_hi, a_hi, start=start, stop=False, skip_group_check=True)
                nc.tensor.matmul(o, w_lo, a_hi, start=False, stop=False, skip_group_check=True)
                return nc.tensor.matmul(o, w_hi, a_lo, start=False, stop=stop, skip_group_check=True)

            M = bank["M"]

            filled = {}

            def x_T(s, b):
                if "M" in filled:
                    sig, before, n_read = filled["M"]
                    pe.wait_ge(sig.sem, sig.at(before, n_read))
                filled["M"] = (xT_split[s], b, 1)
                wait_stage_in(pe, s, b)
                for blk in range(2):
                    m = pe.transpose(M[:, blk * D:(blk + 1) * D], stage_in(s)[b.p][:, blk, :], ident[:, :])
                m.then_inc(xT_ps[s].sem, 1)

            def qk(L, b):
                if "M" in filled:
                    sig, before, n_read = filled["M"]
                    pe.wait_ge(sig.sem, sig.at(before, n_read))
                filled["M"] = (qk_kept[L], b, qk_kept[L].per)
                pe.wait_ge(xT_split[2 * L].sem, xT_split[2 * L].at(b, 2))
                for side in range(2):
                    w = slice(side * D, (side + 1) * D)
                    m = product3(M[:, side * T:(side + 1) * T], wqk_hi[:, L, w], wqk_lo[:, L, w],
                                 xTh[0][:, :], xTl[0][:, :], True, True)
                m.then_inc(qk_ps[L].sem, 1)

            def v(L, b):
                if "M" in filled:
                    sig, before, n_read = filled["M"]
                    pe.wait_ge(sig.sem, sig.at(before, n_read))
                filled["M"] = (v_kept[L], b, 1)
                pe.wait_ge(xT_kept[2 * L].sem, xT_kept[2 * L].at(b, 1))
                for blk in range(2):
                    m = pe.matmul(M[:, blk * D:(blk + 1) * D], xT[:, blk * D:(blk + 1) * D], wvo[:, L, 0, :])
                m.then_inc(v_ps[L].sem, 1)

            def scores(L, b, h):
                k = ("S", "H0", "H1")[h % 3] if L == 0 else ("S", "H1")[h % 2]
                S = bank[k]
                if k in filled:
                    sig, before, n_read = filled[k]
                    pe.wait_ge(sig.sem, sig.at(before, n_read))
                filled[k] = (maxed[L], b, h + 1)
                if h == 0:
                    pe.wait_ge(stacked[L].sem, stacked[L].at(b, 6 * DMA))
                if L == 1:
                    for qb in range(2):
                        m = pe.matmul(S[:, qb * T:(qb + 1) * T], Qs[1][0:96, h, qb * D:(qb + 1) * D],
                                      Ks[1][0:96, h, :])
                else:
                    for qb, (o, n) in enumerate(((0, D), (D, 2 * D))):
                        pe.matmul(S[:, o:o + n], Qs[0][0:96, h, qb * D:(qb + 1) * D], Ks[0][0:96, h, 0:n],
                                  start=True, stop=False, skip_group_check=True)
                        m = pe.matmul(S[:, o + n - D:o + n], identb[:, :], masks[:, 0, :],
                                      start=False, stop=True, skip_group_check=True)
                m.then_inc(s_ps[L].sem, 1)

            def max_T(L, b):
                if "M" in filled:
                    sig, before, n_read = filled["M"]
                    pe.wait_ge(sig.sem, sig.at(before, n_read))
                filled["M"] = (m_parts[L], b, 2)
                pe.wait_ge(maxed[L].sem, maxed[L].at(b, maxed[L].per))
                for qb in range(2):
                    m = pe.transpose(M[0:NH, qb * D:(qb + 1) * D], mp[L][:, qb, :], ident[:, :])
                m.then_inc(mT_ps[L].sem, 1)

            def scores_T(L, b, h):
                k = ("ST0", "ST1")[h % 2]
                S = bank[k]
                if k in filled:
                    sig, before, n_read = filled[k]
                    pe.wait_ge(sig.sem, sig.at(before, n_read))
                filled[k] = (exped[L], b, h + 1)
                if h == 0:
                    pe.wait_ge(m_stacked[L].sem, m_stacked[L].at(b, 2 * DMA))
                if L == 1:
                    for kb in range(2):
                        m = pe.matmul(S[:, kb * T:(kb + 1) * T], Ks[1][:, h, kb * D:(kb + 1) * D], Qs[1][:, h, :])
                else:
                    for kb, (o, n) in enumerate(((0, 2 * D), (2 * D, D))):
                        pe.matmul(S[:, o:o + n], Ks[0][:, h, kb * D:(kb + 1) * D], Qs[0][:, h, kb * D:T],
                                  start=True, stop=False, skip_group_check=True)
                        m = pe.matmul(S[:, o:o + D], identb[:, :], masks[:, 1, :],
                                      start=False, stop=True, skip_group_check=True)
                m.then_inc(st_ps[L].sem, 1)

            def weigh_V(L, b, g):
                if "O" in filled:
                    sig, before, n_read = filled["O"]
                    pe.wait_ge(sig.sem, sig.at(before, n_read))
                filled["O"] = (o_kept[L], b, g + 1)
                pe.wait_ge(exped[L].sem, exped[L].at(b, 4 * g + 4))
                if g == 0:
                    pe.wait_ge(v_kept[L].sem, v_kept[L].at(b, 1))
                O = bank["O"]
                for kb in range(2):
                    for j in range(4):
                        h = 4 * g + j
                        w = V[L][:, kb, h * VW:h * VW + 32]
                        if L == 1 or kb == 0:
                            o, a = O[32 * j:32 * j + 32, 0:T], P[:, g % 2, j, kb * T:(kb + 1) * T]
                        else:
                            o, a = O[32 * j:32 * j + 32, D:T], P[:, g % 2, j, T:T + D]
                        m = pe.matmul(o, w, a, start=(kb == 0), stop=(kb == 1), skip_group_check=True)
                m.then_inc(o_ps[L].sem, 1)

            def O_T(L, b, blk):
                k = "M" if blk == 0 else ("H1", "S")[L]
                if k in filled:
                    sig, before, n_read = filled[k]
                    pe.wait_ge(sig.sem, sig.at(before, n_read))
                filled[k] = (o_norm[L], b, 2 * blk + 2)
                if blk == 0:
                    pe.wait_ge(o_kept[L].sem, o_kept[L].at(b, 4))
                for g in range(4):
                    m = pe.transpose(bank[k][:, g * D:(g + 1) * D], OT[:, g, blk * D:(blk + 1) * D], ident[:, :])
                m.then_inc(oT_ps[L].sem, 1)

            def O_back(L, b):
                if "M" in filled:
                    sig, before, n_read = filled["M"]
                    pe.wait_ge(sig.sem, sig.at(before, n_read))
                filled["M"] = (onT_kept[L], b, 1)
                pe.wait_ge(o_norm[L].sem, o_norm[L].at(b, 4))
                for blk in range(2):
                    m = pe.transpose(M[:, blk * D:(blk + 1) * D], On[:, blk, :], ident[:, :])
                m.then_inc(onT_ps[L].sem, 1)

            def out_proj(L, b):
                if "M" in filled:
                    sig, before, n_read = filled["M"]
                    pe.wait_ge(sig.sem, sig.at(before, n_read))
                filled["M"] = (ln[2 * L], b, 1)
                pe.wait_ge(onT_kept[L].sem, onT_kept[L].at(b, 1))
                for blk in range(2):
                    m = pe.matmul(M[:, blk * D:(blk + 1) * D], OnT[:, blk * D:(blk + 1) * D], wvo[:, L, 1, :])
                m.then_inc(proj_ps[L].sem, 1)

            def logits(L, b):
                if "M" in filled:
                    sig, before, n_read = filled["M"]
                    pe.wait_ge(sig.sem, sig.at(before, n_read))
                filled["M"] = (top[L], b, 1)
                pe.wait_ge(xT_kept[2 * L + 1].sem, xT_kept[2 * L + 1].at(b, 1))
                n = EXPERTS[L]
                w = gw[:, 0:E0] if L == 0 else gw[:, E0:E0 + E1]
                for blk in range(2):
                    m = pe.matmul(M[:, blk * n:(blk + 1) * n], xT[:, blk * D:(blk + 1) * D], w)
                m.then_inc(lg_ps[L].sem, 1)

            def weights_T(L, b):
                if "M" in filled:
                    sig, before, n_read = filled["M"]
                    pe.wait_ge(sig.sem, sig.at(before, n_read))
                filled["M"] = (cT_kept[L], b, 1)
                pe.wait_ge(top[L].sem, top[L].at(b, top_ops(L)))
                for blk in range(2):
                    m = pe.transpose(M[:, blk * D:(blk + 1) * D], comb[L][:, blk, :], ident[:, :])
                m.then_inc(cT_ps[L].sem, 1)

            def fc1(L, b, e):
                k = "H0" if L == 0 else ("H0", "H1", "ST0", "ST1")[e % 4]
                H = bank[k]
                if k in filled:
                    sig, before, n_read = filled[k]
                    pe.wait_ge(sig.sem, sig.at(before, n_read))
                filled[k] = ((acted[0], timed)[L], b, (2 - L) * (e + 1))
                if is_first(b) and L == 0 and e == 0:
                    pe.wait_ge(w_lo_done.sem, NPIECES)
                if e == 0:
                    pe.wait_ge(xT_split[2 * L + 1].sem, xT_split[2 * L + 1].at(b, 2))
                for c in range(2):
                    m = product3(H[:, c * T:(c + 1) * T], w1_hi[L][:, e, c, :], w1_lo[L][:, e, c, :],
                                 xTh[1 + L][:, :], xTl[1 + L][:, :], True, True)
                m.then_inc(h_ps[L].sem, 1)

            def fc2(L, b, e):
                if e == 0:
                    if "Y" in filled:
                        sig, before, n_read = filled["Y"]
                        pe.wait_ge(sig.sem, sig.at(before, n_read))
                    filled["Y"] = (y_kept[L], b, 1)
                pe.wait_ge(lo_done[L].sem, lo_done[L].at(b, e + 1))
                pe.wait_ge(hi_done[L].sem, hi_done[L].at(b, e + 1))
                for c in range(2 - L):
                    s = 2 * (e % 3) + c if L == 0 else e % 6
                    m = product3(bank["Y"][:, 0:T], w2_hi[L][:, e, c, :], w2_lo[L][:, e, c, :],
                                 Ah[:, s, :], Al[:, s, :], e == 0 and c == 0, False)
                m.then_inc(fc2_ps[L].sem, 1)

            def fc2_bias(L, b):
                pe.wait_ge(cT_kept[L].sem, cT_kept[L].at(b, 1))
                pe.matmul(bank["Y"][:, 0:T], b2[:, L, :], combT[L][:, :], start=False, stop=True,
                          skip_group_check=True).then_inc(y_ps[L].sem, 1)

            def y_T(L, b):
                if "M" in filled:
                    sig, before, n_read = filled["M"]
                    pe.wait_ge(sig.sem, sig.at(before, n_read))
                filled["M"] = (ln[2 * L + 1], b, 1)
                pe.wait_ge(y_kept[L].sem, y_kept[L].at(b, 1))
                for blk in range(2):
                    m = pe.transpose(M[:, blk * D:(blk + 1) * D], yT[:, blk * D:(blk + 1) * D], ident[:, :])
                m.then_inc(yT_ps[L].sem, 1)

            def step(name, L, b, x):
                if name == "x_T":
                    x_T(L, b)
                if name == "qk":
                    qk(L, b)
                if name == "v":
                    v(L, b)
                if name == "scores":
                    scores(L, b, x)
                if name == "max_T":
                    max_T(L, b)
                if name == "scores_T":
                    scores_T(L, b, x)
                if name == "weigh_V":
                    weigh_V(L, b, x)
                if name == "O_T":
                    O_T(L, b, x)
                if name == "O_back":
                    O_back(L, b)
                if name == "out_proj":
                    out_proj(L, b)
                if name == "logits":
                    logits(L, b)
                if name == "weights_T":
                    weights_T(L, b)
                if name == "fc1":
                    fc1(L, b, x)
                if name == "fc2":
                    fc2(L, b, x)
                if name == "fc2_bias":
                    fc2_bias(L, b)
                if name == "y_T":
                    y_T(L, b)

            for t in range(FIRST, LOOP_FROM):
                for name, L, k, x in plan_of(t):
                    if active(t, k):
                        step(name, L, Batch(None, t - k), x)
            with pe.Fori(0, (LOOP_TO - LOOP_FROM) // 2) as reg:
                for k, (sig, before, n) in filled.items():
                    filled[k] = (sig, Batch(reg, before.c), n)
                for w in range(2):
                    for name, L, k, x in PLANS["full"]:
                        step(name, L, Batch(reg, LOOP_FROM + w - k), x)
            for k, (sig, before, n) in filled.items():
                filled[k] = (sig, Batch(None, before.c + LOOP_TO - LOOP_FROM - 2), n)
            for t in range(LOOP_TO, LAST + 1):
                for name, L, k, x in plan_of(t):
                    if active(t, k):
                        step(name, L, Batch(None, t - k), x)

        @block.vector
        def _(dve):
            dve.wait_ge(w_in.sem, SMALL_LOADS * DMA)
            dve.tensor_copy(identb[:, :], ident[:, :]).then_inc(const_dve.sem, 1)

            def weights_lo(first, last):
                for i in range(first, last):
                    _, a, z, hi, lo, mult = weight_pieces[i]
                    w = stage[i % STAGES][:, 0:z - a]
                    dve.wait_ge(wst_in[i % STAGES].sem, (i // STAGES + 1) * DMA)
                    if mult:
                        units = slice(C_MULT + a // D, C_MULT + z // D)
                        w3 = w.rearrange("p (u n) -> p u n", n=D)
                        dve.tensor_tensor(w3, w3, cols[:, units].unsqueeze(2).broadcast_to((D, (z - a) // D, D)),
                                          ALU.mult).then_inc(w_scaled.sem, 1)
                        dve.wait_ge(w_scaled.sem, scaled_before[i])
                    dve.wait_ge(w_hi_done.sem, i + 1)
                    dve.tensor_tensor(lo, w, hi.bitcast(F32), ALU.subtract).then_inc(w_lo_done.sem, 1)

            weights_lo(0, 1)
            dve.wait_ge(const_dve.sem, 1)

            M = bank["M"]

            def x_T_lo(s, b):
                dve.wait_ge(xT_split[s].sem, xT_split[s].at(b, 1))
                dve.tensor_tensor(xTl[split_of(s)][:, :], xT[:, :], xTh[split_of(s)][:, :].bitcast(F32),
                                  ALU.subtract).then_inc(xT_split[s].sem, 1)

            def qk_part(L, b, j):
                dve.wait_ge(qk_parts[L].sem, qk_parts[L].at(b, j))
                if j == 2:
                    ins = dve.tensor_copy(parts[:, 1, :], u[:, :])
                elif j == 1:
                    ins = dve.tensor_tensor(u[:, :], u[:, :], parts[:, 0, :], ALU.subtract)
                else:
                    ins = dve.tensor_tensor(parts[:, 2, :], u[:, :], parts[:, 1, :], ALU.subtract)
                ins.then_inc(qk_parts[L].sem, 1)

            def v_keep(L, b):
                dve.wait_ge(v_ps[L].sem, v_ps[L].at(b, 1))
                if is_first(b):
                    dve.wait_ge(const_pool.sem, const_of_layer[L])
                if b.after(1):
                    dve.wait_ge(o_ps[L].sem, o_ps[L].at(b, 4, back=1))
                for blk in range(2):
                    o = V[L][:, blk, 0:NH * VW].rearrange("p (h w) -> p h w", w=VW)[:, :, 0:HD]
                    a = M[:, blk * D:(blk + 1) * D].rearrange("p (h w) -> p h w", w=HD)
                    if L == 0:
                        ins = dve.tensor_copy(o, a)
                    else:
                        ins = dve.tensor_tensor(o, a, rows[:, R_BV:R_BV + D].rearrange("p (h w) -> p h w", w=HD), ALU.add)
                ins.then_inc(v_kept[L].sem, 1)

            def row_max(L, b, h):
                dve.wait_ge(s_ps[L].sem, s_ps[L].at(b, h + 1))
                if h == 0:
                    if b.after(1):
                        dve.wait_ge(mT_ps[L].sem, mT_ps[L].at(b, 1, back=1))
                S = bank[("S", "H0", "H1")[h % 3] if L == 0 else ("S", "H1")[h % 2]]
                n = 2 if L == 1 else 3
                w = T if L == 1 else D
                dve.tensor_reduce(mp[L][:, :, h], S[:, 0:n * w].rearrange("p (a c) -> p a c", a=n),
                                  AX.X, ALU.max).then_inc(maxed[L].sem, 1)

            def max_join(L, b):
                if L == 0:
                    dve.wait_ge(maxed[0].sem, maxed[0].at(b, NH))
                    dve.tensor_tensor(mp[0][:, 1, :], mp[0][:, 1, :], mp[0][:, 2, :], ALU.max)\
                        .then_inc(maxed[0].sem, 1)

            def max_parts(L, b):
                dve.wait_ge(mT_ps[L].sem, mT_ps[L].at(b, 1))
                other = Batch(b.reg, b.c + (K_A0PREP - K_A1 if L == 0 else K_A1 - 1 - K_A0PREP))
                if other.exists():
                    dve.wait_ge(m_stacked[1 - L].sem, m_stacked[1 - L].at(other, 2 * DMA))
                if b.after(1):
                    dve.wait_ge(m_stacked[L].sem, m_stacked[L].at(b, 2 * DMA, back=1))
                dve.tensor_scalar(mrow[:, 0, :], M[0:NH, 0:T], -1.0, None, ALU.mult).then_inc(m_parts[L].sem, 1)
                dve.wait_ge(m_parts[L].sem, m_parts[L].at(b, 1))
                dve.scalar_tensor_tensor(out=mrow[:, 1, :], in0=M[0:NH, 0:T], scalar=-1.0, in1=mrow[:, 0, :],
                                         op0=ALU.mult, op1=ALU.subtract).then_inc(m_parts[L].sem, 1)

            def O_inverse(L, b, blk):
                dve.wait_ge(oT_ps[L].sem, oT_ps[L].at(b, blk + 1))
                O = M if blk == 0 else bank[("H1", "S")[L]]
                dve.reciprocal(oinv[:, blk, :], O[:, :].rearrange("p (h w) -> p h w", w=32)[:, :, HD])\
                    .then_inc(o_norm[L].sem, 1)

            def O_norm(L, b, blk):
                dve.wait_ge(o_norm[L].sem, o_norm[L].at(b, 2 * blk + 1))
                O = M if blk == 0 else bank[("H1", "S")[L]]
                dve.tensor_tensor(On[:, blk, :].rearrange("p (h w) -> p h w", w=HD),
                                  O[:, :].rearrange("p (h w) -> p h w", w=32)[:, :, 0:HD],
                                  oinv[:, blk, :].unsqueeze(2).broadcast_to((D, NH, HD)), ALU.mult)\
                    .then_inc(o_norm[L].sem, 1)

            def add_up(site, b):
                if site % 2 == 0:
                    dve.wait_ge(proj_ps[site // 2].sem, proj_ps[site // 2].at(b, 1))
                else:
                    dve.wait_ge(yT_ps[site // 2].sem, yT_ps[site // 2].at(b, 1))
                if site == 0:
                    wait_x(dve, b)
                if site == 2:
                    dve.wait_ge(bias_added.sem, bias_added.at(b, 1))
                if site == 3:
                    if b.after(1):
                        dve.wait_ge(out_stored.sem, out_stored.at(b, DMA, back=1))
                dst = norm_out(site)[b.p]
                dve.tensor_tensor(dst[:, :, :], M[:, 0:T].rearrange("p (c d) -> p c d", c=2),
                                  stage_in(site)[b.p][:, :, :], ALU.add).then_inc(ln[site].sem, 1)

            def stats(site, b, blk):
                dve.wait_ge(ln[site].sem, ln[site].at(b, 1))
                dve.bn_stats(st6[:, site, blk, :], norm_out(site)[b.p][:, blk, :]).then_inc(ln[site].sem, 1)

            def aggregate(site, b, blk):
                dve.wait_ge(ln[site].sem, ln[site].at(b, 2 + blk))
                if blk == 0:
                    if b.after(1):
                        dve.wait_ge(ln_pool[site].sem, ln_pool[site].at(b, 2, back=1))
                take_wait(dve)
                dve.bn_aggr(mv[:, site, blk, :], st6[:, site, blk, :]).then_inc(ln[site].sem, 1)

            def normalise(site, b, blk):
                if blk == 0:
                    dve.wait_ge(ln_pool[site].sem, ln_pool[site].at(b, 2))
                z = norm_out(site)[b.p][:, blk, :]
                dve.tensor_scalar(z, z, mv[:, site, blk, 0:1], rstd[:, site, blk:blk + 1],
                                  ALU.subtract, ALU.mult).then_inc(ln[site].sem, 1)

            def top_step(L, b, j):
                n, k = EXPERTS[L], TOPK[L]
                sig = top[L]
                if j == 0:
                    if is_first(b):
                        dve.wait_ge(const_pool.sem, len(CONSTANTS))
                    dve.wait_ge(lg_ps[L].sem, lg_ps[L].at(b, 1))
                    if b.after(1):
                        dve.wait_ge(gexp[L].sem, gexp[L].at(b, 2, back=1))
                    src = M[:, 0:2 * n].rearrange("p (c e) -> p c e", c=2)
                    if L == 0:
                        dve.tensor_tensor(lg[0][:, :, :], src, rows[:, R_GB:R_GB + E0].unsqueeze(1).broadcast_to((D, 2, E0)),
                                          ALU.add).then_inc(sig.sem, 1)
                    else:
                        dve.tensor_copy(lg[1][:, :, :], src).then_inc(sig.sem, 1)
                elif j in (1, 2):
                    dve.wait_ge(sig.sem, sig.at(b, 1))
                    take_wait(dve)
                    dve.max(m8[L][:, j - 1, :], lg[L][:, j - 1, :]).then_inc(sig.sem, 1)
                elif j == 3:
                    dve.wait_ge(sig.sem, sig.at(b, 3))
                    dve.tensor_scalar(gs[L][:, 0, :], m8[L][:, :, 0], -1.0, None, ALU.mult).then_inc(sig.sem, 1)
                elif j in (4, 5):
                    dve.wait_ge(sig.sem, sig.at(b, j - 2))
                    take_wait(dve)
                    dve.max_index(ix[L][:, j - 4, :], m8[L][:, j - 4, :], lg[L][:, j - 4, :]).then_inc(sig.sem, 1)
                elif j == 6:
                    dve.wait_ge(sig.sem, sig.at(b, 6))
                    dve.tensor_tensor(eq[L][:, :, :, :],
                                      iota[:, 0:n].unsqueeze(1).unsqueeze(1).broadcast_to((D, 2, k, n)),
                                      ix[L][:, :, 0:k].unsqueeze(3).broadcast_to((D, 2, k, n)), ALU.is_equal)\
                        .then_inc(sig.sem, 1)
                elif j == 7:
                    dve.wait_ge(gexp[L].sem, gexp[L].at(b, 2))
                    dve.reciprocal(gs[L][:, 2, :], gs[L][:, 1, :]).then_inc(sig.sem, 1)
                elif j == 8:
                    dve.wait_ge(sig.sem, sig.at(b, 7))
                    dve.tensor_reduce(mk[L][:, :, :], eq[L][:, :, :, :].rearrange("p c k e -> p c e k"), AX.X, ALU.add)\
                        .then_inc(sig.sem, 1)
                elif j == 9:
                    dve.wait_ge(sig.sem, sig.at(b, 8))
                    dve.tensor_tensor(pe_[L][:, :, :], pe_[L][:, :, :],
                                      gs[L][:, 2, :].unsqueeze(2).broadcast_to((D, 2, n)), ALU.mult).then_inc(sig.sem, 1)
                elif j == 10:
                    dve.wait_ge(sig.sem, sig.at(b, 10))
                    if b.after(1):
                        dve.wait_ge(cT_ps[L].sem, cT_ps[L].at(b, 1, back=1))
                    dve.tensor_tensor(comb[L][:, :, 0:n], mk[L][:, :, :], pe_[L][:, :, :], ALU.mult)\
                        .then_inc(sig.sem, 1)
                elif j == 11:
                    dve.wait_ge(sig.sem, sig.at(b, 11))
                    dve.tensor_reduce(gs[1][:, 3, :], comb[1][:, :, 0:n], AX.X, ALU.add).then_inc(sig.sem, 1)
                elif j == 12:
                    dve.wait_ge(sig.sem, sig.at(b, 12))
                    dve.tensor_scalar(gs[1][:, 3, :], gs[1][:, 3, :], 1e-20, None, ALU.add).then_inc(sig.sem, 1)
                elif j == 13:
                    dve.wait_ge(sig.sem, sig.at(b, 13))
                    dve.reciprocal(gs[1][:, 3, :], gs[1][:, 3, :]).then_inc(sig.sem, 1)
                else:
                    dve.wait_ge(sig.sem, sig.at(b, 14))
                    dve.tensor_tensor(comb[1][:, :, 0:n], comb[1][:, :, 0:n],
                                      gs[1][:, 3, :].unsqueeze(2).broadcast_to((D, 2, n)), ALU.mult).then_inc(sig.sem, 1)

            def times(b, e):
                dve.wait_ge(acted[1].sem, acted[1].at(b, e + 1))
                H = bank[("H0", "H1", "ST0", "ST1")[e % 4]]
                if e >= 6:
                    dve.wait_ge(lo_done[1].sem, lo_done[1].at(b, e - 5))
                dve.scalar_tensor_tensor(out=R[:, e % 6, :], in0=H[:, 0:T],
                                         scalar=cols[:, C_FC1 + 2 * e:C_FC1 + 2 * e + 1],
                                         in1=ge[:, (e % 4) * T:(e % 4 + 1) * T], op0=ALU.add, op1=ALU.mult)\
                    .then_inc(timed.sem, 1)

            def act_lo(L, b, e):
                dve.wait_ge(hi_done[L].sem, hi_done[L].at(b, e + 1))
                depth = (3, 6)[L]
                if e >= depth:
                    dve.wait_ge(fc2_ps[L].sem, fc2_ps[L].at(b, e - depth + 1))
                s = slice(2 * (e % 3), 2 * (e % 3) + 2) if L == 0 else slice(e % 6, e % 6 + 1)
                dve.tensor_tensor(Al[:, s, :], R[:, s, :], Ah[:, s, :].bitcast(F32), ALU.subtract)\
                    .then_inc(lo_done[L].sem, 1)

            def step(name, L, b, x):
                if name == "x_T_lo":
                    x_T_lo(L, b)
                if name == "qk_part":
                    qk_part(L, b, x)
                    if L == 0 and x == 3 and is_first(b):
                        weights_lo(1, EARLY_PIECES)
                if name == "v_keep":
                    v_keep(L, b)
                if name == "row_max":
                    row_max(L, b, x)
                if name == "max_join":
                    max_join(L, b)
                if name == "max_parts":
                    max_parts(L, b)
                    if L == 0 and is_first(b):
                        weights_lo(EARLY_PIECES, NPIECES)
                if name == "O_inverse":
                    O_inverse(L, b, x)
                if name == "O_norm":
                    O_norm(L, b, x)
                if name == "sum":
                    add_up(L, b)
                if name == "stats":
                    stats(L, b, x)
                if name == "aggregate":
                    aggregate(L, b, x)
                if name == "normalise":
                    normalise(L, b, x)
                if name == "top":
                    top_step(L, b, x)
                if name == "times":
                    times(b, x)
                if name == "act_lo":
                    act_lo(L, b, x)

            run_slots(dve, step)


def kernel(**inputs):
    import numpy as np
    import concourse.bacc as bacc
    import ml_dtypes
    from concourse.bass_utils import run_bass_kernel_spmd

    a = {k: np.asarray(v) for k, v in inputs.items()}

    def flat(w):
        return np.ascontiguousarray(w.reshape(w.shape[0], -1))

    fc1 = a["L1_ffn_fc1_w"].reshape(E1, 2, D, D)
    s1 = a["L1_ffn_s_fc1_w"].reshape(2, 2, D, D).transpose(1, 0, 2, 3)
    fc1 = np.concatenate([fc1, s1], axis=0)
    fc1b = np.concatenate([a["L1_ffn_fc1_b"].reshape(E1, 2, D),
                           a["L1_ffn_s_fc1_b"].reshape(2, 2, D).transpose(1, 0, 2)], axis=0)
    mult = np.concatenate([a["L1_ffn_geglu_mult"], a["L1_ffn_s_geglu_mult"].reshape(2, D)], axis=0)
    fc2 = np.concatenate([a["L1_ffn_fc2_w"], a["L1_ffn_s_fc2_w"].reshape(D, 2, D).transpose(1, 0, 2)], axis=0)
    w_in = a["L1_attn_w_in"].transpose(1, 0)
    qkv = a["L0_attn_w_qkv"]
    b_in = a["L1_attn_b_in"]
    neg = np.float32(NEG)
    key_after = np.arange(D)[None, :] > np.arange(D)[:, None]
    mask_qk = np.where(key_after, neg, np.float32(0)).astype(ml_dtypes.bfloat16)
    arrays = {
        "x_in": a["L0_attn_x"],
        "cols_in": np.concatenate([a["L0_ffn_b1"].reshape(2 * E0, D).transpose(1, 0),
                                   fc1b.reshape(2 * U1, D).transpose(1, 0), mult.transpose(1, 0),
                                   b_in[0:2 * D].reshape(2, D).transpose(1, 0)], axis=1),
        "rows_in": np.concatenate([a["L0_ffn_gate_b"], b_in[2 * D:], a["L1_attn_b_out"]]),
        "wqk0_in": qkv[:, 0:2 * D],
        "wvo0_in": np.concatenate([qkv[:, 2 * D:], a["L0_attn_w_out"]], axis=1),
        "wqk1_in": w_in[:, 0:2 * D],
        "wvo1_in": np.concatenate([w_in[:, 2 * D:], a["L1_attn_w_out"].transpose(1, 0)], axis=1),
        "gw_in": np.concatenate([a["L0_ffn_gate_w"], a["L1_ffn_gate_w"].transpose(1, 0)], axis=1),
        "w1_0_in": flat(a["L0_ffn_w1"].transpose(1, 0, 2)),
        "w2_0_in": flat(a["L0_ffn_w2"].reshape(E0, 2, D, D).transpose(2, 0, 1, 3)),
        "w1_1_in": flat(fc1.transpose(3, 0, 1, 2)),
        "w2_1_in": flat(fc2.transpose(2, 0, 1)),
        "b2_0_in": a["L0_ffn_b2"],
        "b2_1_in": np.concatenate([a["L1_ffn_fc2_b"], a["L1_ffn_s_fc2_b"].reshape(1, D)], axis=0),
        "ident_in": np.eye(D, dtype=np.float32),
        "masks_in": np.concatenate([mask_qk, mask_qk.transpose(1, 0)], axis=1),
    }
    arrays = {k: np.ascontiguousarray(v) for k, v in arrays.items()}
    nc = bacc.Bacc("TRN2", target_bir_lowering=False, num_devices=1)
    args = {k: nc.dram_tensor(k, v.shape, mybir.dt.from_np(v.dtype), kind="ExternalInput").ap()
            for k, v in arrays.items()}
    out = nc.dram_tensor("out", (NB, T, D), F32, kind="ExternalOutput").ap()
    build(nc, **args, out=out)
    r = run_bass_kernel_spmd(nc, [arrays], core_ids=[0])
    return r.results[0]["out"]
```
